# Optimizing a Trainium2 kernel written in Bass

```python
import numpy as np
import jax
import jax.numpy as jnp

def _softmax(x, axis=-1):
    return jax.nn.softmax(x, axis=axis)

def _gelu(x):
    return jax.nn.gelu(x, approximate=True)

def _silu(x):
    return jax.nn.silu(x)

def _sigmoid(x):
    return jax.nn.sigmoid(x)

def _layernorm(x, axis=-1, eps=1e-05):
    m = jnp.mean(x, axis=axis, keepdims=True)
    v = jnp.var(x, axis=axis, keepdims=True)
    return (x - m) / jnp.sqrt(v + eps)

def _scatter_add(tgt, idx, src, axis=0):
    return tgt.at[idx].add(src)

def _segment_sum(src, seg, n):
    return jax.ops.segment_sum(src, seg, n)
kernel_name = 'mk_adj_ffn_d1_adj_r2_323c2d'

def setup_inputs(seed: int=0):
    np.random.seed(seed)
    _w = jnp.asarray

    def _rec_inputs():
        import jax
        import jax.numpy as jnp
        _gk = jax.random.key(seed)
        x = -0.0003929 + 0.9999 * jax.random.normal(jax.random.fold_in(_gk, 1), (32, 256, 256), jnp.float32)
        _a = jax.random.bernoulli(jax.random.fold_in(_gk, 2), 0.0625, (256, 256))
        _a = jnp.logical_or(_a, jnp.swapaxes(_a, -1, -2))
        _a = jnp.logical_or(_a, jnp.eye(256, dtype=bool))
        _af = _a.astype(jnp.float32)
        _af = _af * jax.random.uniform(jax.random.fold_in(_gk, 3), (256, 256), jnp.float32, 0.05, 1)
        adj = _af
        return (x, adj)
    x, adj = _rec_inputs()

    def _L0_gnn_setup():
        import jax, jax.numpy as jnp
        import numpy as np
        B, N, F_IN, F_OUT = (16, 1024, 256, 256)
        key = jax.random.key(seed)
        k1, k2, k3 = jax.random.split(key, 3)
        x = jax.random.normal(k1, (B, N, F_IN), dtype=jnp.float32)
        adj = jax.random.uniform(k2, (N, N), dtype=jnp.float32)
        bound = np.sqrt(6.0 / F_OUT)
        weight = jax.random.uniform(k3, (F_IN, F_OUT), dtype=jnp.float32, minval=-bound, maxval=bound)
        bias = jnp.zeros((F_OUT,), dtype=jnp.float32)
        return {'x': x, 'adj': adj, 'weight': weight, 'bias': bias}
    _L0_gnn_all = _L0_gnn_setup()
    _L0_gnn_in = {k: v for k, v in _L0_gnn_all.items() if k in ('weight', 'bias')}
    del _L0_gnn_all

    def _L0_ffn_setup():
        import jax, jax.numpy as jnp
        import numpy as np
        TOP_K = 2
        key = jax.random.key(seed)
        ks = jax.random.split(key, 4)
        b, t, d, e, h = (2, 1024, 256, 8, 512)
        scale = 0.02
        return {'x': jax.random.normal(ks[0], (b, t, d), dtype=jnp.float32), 'router_w': jax.random.normal(ks[1], (e, d), dtype=jnp.float32) * scale, 'router_b': jnp.zeros((e,), dtype=jnp.float32), 'fc1_w': jax.random.normal(ks[2], (e, 2 * h, d), dtype=jnp.float32) * scale, 'fc1_b': jnp.zeros((e, 2 * h), dtype=jnp.float32), 'fc2_w': jax.random.normal(ks[3], (e, d, h), dtype=jnp.float32) * scale, 'fc2_b': jnp.zeros((e, d), dtype=jnp.float32)}
    _L0_ffn_all = _L0_ffn_setup()
    _L0_ffn_in = {k: v for k, v in _L0_ffn_all.items() if k in ('router_w', 'router_b', 'fc1_w', 'fc1_b', 'fc2_w', 'fc2_b')}
    del _L0_ffn_all
    return {'x': x, 'adj': adj, 'L0_gnn_weight': _L0_gnn_in['weight'], 'L0_gnn_bias': _L0_gnn_in['bias'], 'L0_ffn_router_w': _L0_ffn_in['router_w'], 'L0_ffn_router_b': _L0_ffn_in['router_b'], 'L0_ffn_fc1_w': _L0_ffn_in['fc1_w'], 'L0_ffn_fc1_b': _L0_ffn_in['fc1_b'], 'L0_ffn_fc2_w': _L0_ffn_in['fc2_w'], 'L0_ffn_fc2_b': _L0_ffn_in['fc2_b']}

def reference(x, adj, L0_gnn_weight, L0_gnn_bias, L0_ffn_router_w, L0_ffn_router_b, L0_ffn_fc1_w, L0_ffn_fc1_b, L0_ffn_fc2_w, L0_ffn_fc2_b):
    import jax
    import jax.numpy as jnp

    def _L0_gnn_ref(x, adj, weight, bias):
        import jax, jax.numpy as jnp
        import numpy as np
        B, N, F_IN, F_OUT = (16, 1024, 256, 256)
        deg = adj.sum(axis=1)
        deg_inv_sqrt = jnp.where(deg > 0, jax.lax.rsqrt(deg), 0.0)
        norm_adj = adj * deg_inv_sqrt[:, None] * deg_inv_sqrt[None, :]
        support = jnp.einsum('bni,io->bno', x, weight)
        output = jnp.einsum('nm,bmo->bno', norm_adj, support)
        return output + bias

    def _L0_ffn_ref(x, router_w, router_b, fc1_w, fc1_b, fc2_w, fc2_b):
        import jax, jax.numpy as jnp
        import numpy as np
        TOP_K = 2
        n_experts = router_w.shape[0]
        temp = 1.0
        logits = (jnp.einsum('btd,ed->bte', x, router_w) + router_b) / temp
        topk_val, topk_idx = jax.lax.top_k(logits, TOP_K)
        weights = jax.nn.softmax(topk_val, axis=-1)
        onehot = jax.nn.one_hot(topk_idx, n_experts, dtype=x.dtype)
        cw = jnp.einsum('btk,btke->bte', weights, onehot)
        h = jnp.einsum('btd,efd->btef', x, fc1_w) + fc1_b
        h1, h2 = jnp.split(h, 2, axis=-1)
        a = jax.nn.silu(h1) * h2
        y = jnp.einsum('bteh,edh->bted', a, fc2_w) + fc2_b
        out = jnp.einsum('bted,bte->btd', y, cw)
        return out
    x = x + _L0_gnn_ref(_layernorm(x, axis=-1), adj, L0_gnn_weight, L0_gnn_bias)
    x = x + _L0_ffn_ref(_layernorm(x, axis=-1), L0_ffn_router_w, L0_ffn_router_b, L0_ffn_fc1_w, L0_ffn_fc1_b, L0_ffn_fc2_w, L0_ffn_fc2_b)
    return x

_drawn_inputs = setup_inputs


def setup_inputs(seed=0):
    import zlib

    import numpy as np

    out = dict(_drawn_inputs(seed))
    spreads = {'L0_gnn_bias': (0.0, 0.1),
     'L0_ffn_router_b': (0.0, 0.1),
     'L0_ffn_fc1_b': (0.0, 0.8),
     'L0_ffn_fc2_b': (0.0, 0.1)}
    factors = {'L0_ffn_fc1_w': 3.167, 'L0_ffn_fc2_w': 3.147}
    for name, (base, spread) in spreads.items():
        noise = np.random.default_rng([zlib.crc32(name.encode()), seed]).standard_normal(out[name].shape)
        drawn = base * np.exp(spread * noise) if base else spread * noise
        out[name] = jnp.asarray(drawn.astype(out[name].dtype))
    for name, factor in factors.items():
        out[name] = (out[name] * factor).astype(out[name].dtype)
    return out
```

```python
from contextlib import ExitStack

import concourse.bass as bass
from concourse import mybir

F32 = mybir.dt.float32
F16 = mybir.dt.float16
I32 = mybir.dt.int32
ALU = mybir.AluOpType
ACT = mybir.ActivationFunctionType
AX = mybir.AxisListType

P = 128
D = 256
DK = D // P
BATCHES = 32
NODES = 256
J = NODES // P
TOKENS = BATCHES * NODES
E = 8
H = 512
HK = H // P
FT = 2 * H // P
BLOCK = 256
MAX_BLOCKS = (2 * TOKENS + E * (BLOCK - 1)) // BLOCK
GROUP = 4
TILES = GROUP * J
GROUPS = BATCHES // GROUP
TABLE = E * TOKENS + MAX_BLOCKS * BLOCK
ROW = 2 * D + 2 * E
W1N = DK * 2 * H
W2N = HK * D
EPS = 1e-5
TOP = 2.0 ** 14
S1, I1, C2, S2, CY = range(5)

IDX_RING = 8
AHEAD = 3
NCHAIN = 11
NROUTE = 18


def program(nc, x, adj, adj_t, gnn_w, gnn_b, router_w, router_b, w1, b1, w2, b2, out):
    x_v = x.rearrange("(b j p) d -> b p j d", j=J, p=P)
    out_v = out.rearrange("(b j p) d -> b p j d", j=J, p=P)
    rows = nc.dram_tensor("rows", (TOKENS + BLOCK, ROW // 2), I32, kind="Internal").ap()
    rows_v = rows.rearrange("(g t p) c -> g p t c", t=2, p=P)
    table = nc.dram_tensor("table", (TABLE, 1), I32, kind="Internal").ap()
    table_b = table.rearrange("(b p j) o -> b p (j o)", p=P, j=2)

    with ExitStack() as ctx:
        def sb(name, shape, dt=F32):
            return ctx.enter_context(nc.sbuf_tensor(name, shape, dt))

        def sem(name):
            return ctx.enter_context(nc.semaphore(name))

        bank = [ctx.enter_context(nc.psum_tensor(f"bank{i}", [P, 512], F32)) for i in range(8)]

        W1 = sb("W1", [P, E, 2, DK, 2 * H], F16)
        W2 = sb("W2", [P, E, 2, HK, D], F16)
        stage = sb("stage", [P, 2, W1N + W2N])
        ident = sb("ident", [P, P], F16)
        tri = sb("tri", [P, P], F16)
        ones = sb("ones", [P, P], F16)
        eps = sb("eps", [P, 1])
        ids = sb("ids", [P, BATCHES * J], I32)
        iota_i = sb("iota_i", [P, 2, TILES, E], I32)
        rev = sb("rev", [P, TILES, E])
        ebase = sb("ebase", [P, TILES, E])
        steps_i = sb("steps_i", [1, 32 + MAX_BLOCKS], I32)
        steps_f = sb("steps_f", [1, 32 + MAX_BLOCKS])
        pad_out = sb("pad_out", [P, TABLE // P], I32)
        zeros = sb("zeros", [P, 2, ROW // 2], I32)
        ones8 = sb("ones8", [1, E])
        adj_n = sb("adj_n", [P, J, NODES])
        At = sb("At", [P, J, NODES])
        Wg = sb("Wg", [P, DK, D])
        bg = sb("bg", [P, D])
        rw = sb("rw", [P, DK, E])
        rw16 = sb("rw16", [P, 2, DK, E], F16)
        rb = sb("rb", [P, E])
        b1t = sb("b1t", [P, E, FT])
        b2t = sb("b2t", [P, E, D])
        deg = sb("deg", [P, 5, J])
        dinv = sb("dinv", [P, J])
        xin = sb("xin", [P, 4, J, D])
        xb = sb("xb", [P, 4, J, D])
        st = sb("st", [P, 2, 2 * J, 6])
        mv = sb("mv", [P, 2, 2 * J, 2])
        sd = sb("sd", [P, 2, 2 * J])
        rs = sb("rs", [P, 2, 2 * J])
        xn1 = sb("xn1", [P, 2, J, D])
        ts = sb("ts", [P, 2, DK, NODES])
        x2 = sb("x2", [P, 4, J, D])
        xn2 = sb("xn2", [P, 2, J, D])
        xrow = sb("xrow", [P, 2 * GROUP, J, ROW], F16)
        xT = sb("xT", [P, 2, 2, DK, NODES], F16)
        pad_ids = xT[:].rearrange("p a l k n -> p (a l k n)").bitcast(I32)[:, 0:TABLE // P]
        lg = sb("lg", [P, 2, TILES, E])
        m12 = sb("m12", [P, 5, TILES])
        ra = sb("ra", [P, 6, TILES, E])
        M = sb("M", [P, 2, TILES, E], F16)
        Mg = sb("Mg", [P, E])
        Macc = sb("Macc", [P, 2, E], F16)
        gids = sb("gids", [P, 2, TILES], I32)
        slots = sb("slots", [P, 2, 2, TILES], I32)
        am = sb("am", [P, 2, 9])
        ar = sb("ar", [P, 2, 9])
        v = sb("v", [P, 3])
        pw = sb("pw", [P, 3])
        rp = sb("rp", [P, 3])
        K = sb("K", [P, E, 5])
        beta = sb("beta", [P, E, HK])
        nb = sb("nb", [1, 4, E])
        spare = xin[0:1].rearrange("p a j d -> p (a j d)")
        cmp1 = spare[:, 1536:1536 + 32 * E].rearrange("p (e s) -> p e s", e=E)
        cmp2 = spare[:, 0:2 * MAX_BLOCKS * E].rearrange("p (a b e) -> p a b e", a=2, e=E)
        bl = sb("bl", [1, 4, MAX_BLOCKS])
        info = sb("info", [1, 2, MAX_BLOCKS + 1], I32)
        idx = sb("idx", [P, IDX_RING, 2], I32)
        G = xrow[:, 0:4]
        XT = xn1[:].rearrange("p a j d -> p (a j d)").bitcast(F16).rearrange("p (a l k n) -> p a l k n", a=2, l=2, k=DK)
        free = stage[:].rearrange("p a n -> p (a n)")
        N = HK * BLOCK
        act1 = free[:, 0:N].rearrange("p (f n) -> p f n", f=HK)
        prod = free[:, N:3 * N].rearrange("p (a f n) -> p a f n", a=2, f=HK)
        ab = free[:, 3 * N:5 * N].bitcast(F16).rearrange("p (a l f n) -> p a l f n", a=2, l=2, f=HK)
        th = sb("th", [P, 2, 2])
        cw = sb("cw", [P, 2, 2])
        y1 = xb[:, 0:2]
        y2 = x2[:, 0:2]

        def g_bank(b2):
            return bank[2 + b2][:].rearrange("p (j d) -> p j d", j=J)

        xTp = bank[4][:].bitcast(F16).rearrange("p (l k n) -> p l k n", l=2, k=DK)
        lgp = bank[5][:, 0:J * E].rearrange("p (j e) -> p j e", j=J)
        rkp = bank[6][:, 0:TILES * E].rearrange("p (t e) -> p t e", t=TILES)
        totp = bank[7][:, 0:E]
        b1v = b1t[:]

        small_in = sem("small_in")
        x_in = [sem(f"x_in{i}") for i in range(4)]
        w_in = [sem(f"w_in{i}") for i in range(2)]
        const_pool = sem("const_pool")
        const_dve = sem("const_dve")
        deg_root = sem("deg_root")
        pad_stored = sem("pad_stored")
        xb_ready = sem("xb_ready")
        bn1 = sem("bn1")
        bn2 = sem("bn2")
        mv1 = sem("mv1")
        mv2 = sem("mv2")
        sd_ready = sem("sd_ready")
        rs_ready = sem("rs_ready")
        xn1_ready = sem("xn1_ready")
        t_ready = sem("t_ready")
        ts_ready = sem("ts_ready")
        g_ready = sem("g_ready")
        x2_ready = sem("x2_ready")
        x2_stored = [sem(f"x2_stored{i}") for i in range(4)]
        xn2_ready = sem("xn2_ready")
        hi_ready = sem("hi_ready")
        lo_ready = sem("lo_ready")
        xTp_ready = sem("xTp_ready")
        xT_ready = sem("xT_ready")
        lgp_ready = sem("lgp_ready")
        lg_ready = sem("lg_ready")
        route = sem("route")
        rank_ready = sem("rank_ready")
        row_stored = [sem(f"row_stored{i}") for i in range(2)]
        scattered = [sem(f"scattered{i}") for i in range(2)]
        am_ready = sem("am_ready")
        ar_ready = sem("ar_ready")
        scale = sem("scale")
        whi_ready = sem("whi_ready")
        wlo_ready = sem("wlo_ready")
        tot_ready = sem("tot_ready")
        blk = sem("blk")
        idx_in = [sem(f"idx_in{i}") for i in range(IDX_RING)]
        g_in = [sem(f"g_in{i}") for i in range(4)]
        XTp_ready = sem("XTp_ready")
        XT_ready = sem("XT_ready")
        h_ready = sem("h_ready")
        act_ready = sem("act_ready")
        prod_ready = sem("prod_ready")
        ahi_ready = sem("ahi_ready")
        alo_ready = sem("alo_ready")
        y_ready = sem("y_ready")
        y1_ready = sem("y1_ready")
        th_ready = sem("th_ready")
        cw_ready = sem("cw_ready")
        y2_ready = sem("y2_ready")
        added = sem("added")

        block = ctx.enter_context(nc.Block())

        LAST = BATCHES + 2 * GROUP // 2 + 2

        def phase_a(eng, step):
            for i in range(8):
                step(i, i, i // GROUP)
            with eng.Fori(8 // GROUP, GROUPS - 1, 2) as g0:
                for u in range(8):
                    step(g0 * GROUP + u, 8 + u, g0 + u // GROUP)
            for i in range(BATCHES, LAST):
                step(i, i, i // GROUP)

        def live(s, back, n=BATCHES):
            return back <= s < n + back

        def hold(eng, sem, value):
            if not isinstance(value, int):
                value = eng.to_reg(value)
                eng.wait_ge(sem, 1)
            eng.wait_ge(sem, value)

        def bufcount(b, s):
            if isinstance(b, int):
                return 16 * ((b // GROUP) // 2)
            return (b - (s % 8)) * 2

        def kcol(e, c):
            return K[:, bass.ds(e, 1), c:c + 1].rearrange("p a c -> p (a c)")

        def w1q(e, part, u):
            return W1[:].rearrange("p e l k f -> p e l (k f)")[:, bass.ds(e, 1), part, u * 512:(u + 1) * 512].rearrange("p a n -> p (a n)")

        def w2q(e, part, u):
            return W2[:].rearrange("p e l k f -> p e l (k f)")[:, bass.ds(e, 1), part, u * 256:(u + 1) * 256].rearrange("p a n -> p (a n)")

        def phase_b(eng, front, back):
            front(0, 0)
            n = 4
            for b in range(1, n):
                front(b, b)
                back(b - 1, b - 1)
            with eng.Fori(n, (MAX_BLOCKS - n) // 4 * 4 + 1, 4) as b0:
                for k in range(4):
                    front(b0 + k, n + k)
                    back(b0 + k - 1, n + k - 1)
            for b in range(n + (MAX_BLOCKS - n) // 4 * 4, MAX_BLOCKS):
                front(b, b)
                back(b - 1, b - 1)
            back(MAX_BLOCKS - 1, MAX_BLOCKS - 1)

        @block.sync
        def _(sp):
            for dst, src in ((adj_n, adj), (At, adj_t), (Wg, gnn_w), (rw, router_w), (b1t, b1)):
                sp.dma_start(dst[:], src).then_inc(small_in, 16)
            sp.dma_start(bg[:], gnn_b.rearrange("(a d) -> a d", a=1).broadcast_to([P, D])).then_inc(small_in, 16)
            sp.dma_start(rb[:], router_b.rearrange("(a d) -> a d", a=1).broadcast_to([P, E])).then_inc(small_in, 16)
            sp.dma_start(b2t[:], b2.rearrange("(a e) d -> a e d", a=1).broadcast_to([P, E, D])).then_inc(small_in, 16)

            def load_w(g, n):
                sp.dma_start(stage[:, n % 2, 0:W1N], w1[bass.ds(g, 1)].rearrange("a p n -> p (a n)")).then_inc(w_in[n % 2], 16)
                sp.dma_start(stage[:, n % 2, W1N:], w2[bass.ds(g, 1)].rearrange("a p n -> p (a n)")).then_inc(w_in[n % 2], 16)

            def step(i, s, g):
                if live(s, 0):
                    if s >= 4:
                        hold(sp, x2_ready, (i - 3) * J)
                    sp.dma_start(xin[:, s % 4], x_v[bass.ds(i, 1)].rearrange("a p j d -> p (a j) d")).then_inc(x_in[s % 4], 16)
                if s % GROUP == 0 and live(s, 0):
                    if s >= 2 * GROUP:
                        sp.wait_ge(whi_ready, (g - 1) * 8)
                        hold(sp, wlo_ready, (g - 1) * 8)
                    load_w(g, (s // GROUP) % 2)
                if live(s, 3):
                    hold(sp, x2_ready, (i - 2) * J)
                    sp.dma_start(out_v[bass.ds(i - 3, 1)].rearrange("a p j d -> p (a j) d"), x2[:, (s - 3) % 4]).then_inc(x2_stored[(s - 3) % 4], 16)
                if s % GROUP == 1 and live(s, 9):
                    hold(sp, route, (g - 2) * NROUTE + 14)
                    hold(sp, lo_ready, (g - 1) * GROUP)
                    q = (s // GROUP) % 2
                    sp.dma_start(rows_v[bass.ds((g - 2) * GROUP, GROUP)].rearrange("b p j c -> p b j c"),
                                 xrow[:, q * GROUP:(q + 1) * GROUP].bitcast(I32)).then_inc(row_stored[q], 16)
            sp.wait_ge(const_pool, 8)
            sp.dma_start(rows_v[BATCHES], zeros[:]).then_inc(pad_stored, 16)
            sp.dma_start(out_v[BATCHES], zeros[:, :, 0:D].bitcast(F32)).then_inc(pad_stored, 16)
            phase_a(sp, step)

            for s in scattered:
                sp.wait_ge(s, 16 + 16 * 2 * TILES * GROUPS // 2)
            sp.wait_ge(blk, 12)

            def load_idx(b, k):
                start = sp.value_load(info[0:1, 1, bass.ds(b, 1)], min_val=0, max_val=TABLE // BLOCK - 1)
                sp.dma_start(idx[:, k], table_b[bass.ds(start, 1)].rearrange("a p j -> p (a j)")).then_inc(idx_in[k], 16)

            for b in range(IDX_RING):
                load_idx(b, b)
            full = MAX_BLOCKS // IDX_RING * IDX_RING
            with sp.Fori(IDX_RING, full, IDX_RING) as b0:
                for k in range(IDX_RING):
                    hold(sp, added, (b0 + k - IDX_RING + 1) * 32)
                    load_idx(b0 + k, k)
            for b in range(full, MAX_BLOCKS):
                sp.wait_ge(added, (b - IDX_RING + 1) * 32)
                load_idx(b, b % IDX_RING)
            sp.wait_ge(added, MAX_BLOCKS * 32)

        @block.gpsimd
        def _(pool):
            pool.memset(zeros[:], 0).then_inc(const_pool, 1)
            pool.memset(ones[:], 1.0).then_inc(const_pool, 1)
            pool.iota(pad_ids, pattern=[[1, TABLE // P]], base=0, channel_multiplier=TABLE // P).then_inc(const_pool, 1)
            pool.iota(ids[:], pattern=[[P, BATCHES * J]], base=0, channel_multiplier=1).then_inc(const_pool, 1)
            pool.iota(iota_i[:, 0], pattern=[[0, TILES], [-1, E]], base=E, channel_multiplier=0).then_inc(const_pool, 1)
            pool.iota(iota_i[:, 1], pattern=[[0, TILES], [TOKENS, E]], base=0, channel_multiplier=0).then_inc(const_pool, 1)
            pool.iota(steps_i[:, 0:32], pattern=[[BLOCK, 32]], base=0, channel_multiplier=0).then_inc(const_pool, 1)
            pool.iota(steps_i[:, 32:], pattern=[[1, MAX_BLOCKS]], base=0, channel_multiplier=0).then_inc(const_pool, 1)
            pool.wait_ge(const_pool, 8)
            pool.affine_select(out=tri[:], in_=ones[:], pattern=[[1, P]], compare_op=ALU.is_gt, fill=0.0,
                               base=0, channel_multiplier=-1).then_inc(const_pool, 1)
            pool.affine_select(out=ident[:], in_=ones[:], pattern=[[1, P]], compare_op=ALU.is_equal, fill=0.0,
                               base=0, channel_multiplier=-1).then_inc(const_pool, 1)
            pool.wait_ge(small_in, 16 * 8)
            pool.wait_ge(const_dve, 12)
            half = TABLE // P // 2
            for q in range(2):
                pool.dma_start(table.rearrange("(p c) o -> p (c o)", p=P)[:, q * half:(q + 1) * half],
                             pad_out[:, q * half:(q + 1) * half]).then_inc(scattered[q], 16)
            for q in scattered:
                pool.wait_ge(q, 16)

            def scatter(i, s, g, c):
                q = (s // GROUP) % 2
                for k in range(2):
                    pool.indirect_dma_start(
                        table, bass.IndirectOffsetOnAxis(ap=slots[:, q, k, c:c + 1], axis=0),
                        gids[:, q, c:c + 1], None).then_inc(scattered[q], 16)

            def step(i, s, g):
                if live(s, 0):
                    pool.wait_ge(x_in[s % 4], (i - s % 4) * 4 + 16 if s % 4 else i * 4 + 16)
                    if s >= 4:
                        pool.wait_ge(x2_ready, (i - 3) * J)
                    pool.tensor_tensor(xb[:, s % 4], xin[:, s % 4], bg[:].rearrange("p (a d) -> p a d", a=1).broadcast_to([P, J, D]), ALU.add).then_inc(xb_ready, 1)
                if s % GROUP == 3 and live(s, 0):
                    hold(pool, am_ready, (g + 1) * 9)
                    q = (s // GROUP) % 2
                    pool.partition_all_reduce(ar[:, q], am[:, q], P, bass.bass_isa.ReduceOp.max).then_inc(ar_ready, 1)
                if s % GROUP in (2, 3) and live(s - s % GROUP, 8):
                    if s % GROUP == 2:
                        hold(pool, route, (g - 1) * NROUTE)
                    for c in range((s % GROUP - 2) * 4, (s % GROUP - 1) * 4):
                        scatter(i, s, g - 2, c)
            phase_a(pool, step)
            pool.wait_ge(route, GROUPS * NROUTE)
            for c in range(TILES if LAST % GROUP <= 2 else 0):
                scatter(LAST, (GROUPS + 1) * GROUP, GROUPS - 1, c)

            pool.wait_ge(pad_stored, 16 * 2)
            for s in row_stored:
                pool.wait_ge(s, 16 * GROUPS // 2)
            for s in x2_stored:
                pool.wait_ge(s, 16 * BATCHES // 4)

            def gather(b, k):
                hold(pool, idx_in[k % IDX_RING], (b - k % IDX_RING) * 2 + 16)
                if k >= 4:
                    hold(pool, XTp_ready, b - 3)
                    pool.wait_ge(th_ready, b - 3)
                for j in range(J):
                    pool.indirect_dma_start(G[:, k % 4, j].bitcast(I32), None, rows,
                                            bass.IndirectOffsetOnAxis(ap=idx[:, k % IDX_RING, j:j + 1], axis=0)).then_inc(g_in[k % 4], 16)

            def add(b, k):
                pool.wait_ge(y2_ready, (b + 1) * J)
                if k >= 1:
                    hold(pool, added, b * 32)
                for j in range(J):
                    pool.indirect_dma_start(out, bass.IndirectOffsetOnAxis(ap=idx[:, k % IDX_RING, j:j + 1], axis=0),
                                            y2[:, k % 2, j], None, compute_op=ALU.add).then_inc(added, 16)

            for b in range(AHEAD + 1):
                gather(b, b)
            add(0, 0)
            first = AHEAD + 1
            full = (MAX_BLOCKS - first) // IDX_RING * IDX_RING + first
            with pool.Fori(first, full, IDX_RING) as b0:
                for k in range(IDX_RING):
                    gather(b0 + k, first + k)
                    add(b0 + k - AHEAD, first + k - AHEAD)
            for b in range(full, MAX_BLOCKS):
                gather(b, b)
                add(b - AHEAD, b - AHEAD)
            for b in range(MAX_BLOCKS - AHEAD, MAX_BLOCKS):
                add(b, b)

        @block.scalar
        def _(act):
            act.wait_ge(const_dve, 5)
            act.activation(deg[:, 3], deg[:, 2], ACT.Sqrt).then_inc(deg_root, 1)

            def step(i, s, g):
                p = s % 2
                if live(s, 3):
                    act.wait_ge(xn2_ready, (i - 2) * J)
                    if s - 3 >= 2 * GROUP and (s - 3) % GROUP == 0:
                        act.wait_ge(row_stored[((s - 3) // GROUP) % 2], bufcount(i - 3, s - 3))
                    act.activation(xrow[:, (s - 3) % 8, :, 0:D], xn2[:, (s - 3) % 2], ACT.Copy).then_inc(hi_ready, 1)
                if live(s, 1):
                    act.wait_ge(t_ready, i)
                    if s >= 3:
                        act.wait_ge(g_ready, i - 2)
                    act.activation(ts[:, (s - 1) % 2], bank[(s - 1) % 2][:].rearrange("p (k n) -> p k n", k=DK), ACT.Copy).then_inc(ts_ready, 1)
                if live(s, 4):
                    act.wait_ge(xTp_ready, i - 3)
                    if s >= 6:
                        act.wait_ge(lgp_ready, i - 5)
                    act.activation(xT[:, s % 2], xTp, ACT.Copy).then_inc(xT_ready, 1)
                if live(s, 0) or live(s, 2):
                    a, z = (0 if live(s, 0) else J), (2 * J if live(s, 2) else J)
                    if live(s, 0):
                        act.wait_ge(mv1, (i + 1) * J)
                    if live(s, 2):
                        act.wait_ge(mv2, (i - 1) * J)
                    if s == 0:
                        act.wait_ge(const_dve, 1)
                    if s >= 2:
                        act.wait_ge(rs_ready, i - 1)
                    act.activation(sd[:, p, a:z], mv[:, p, a:z, 1], ACT.Sqrt, bias=eps[:]).then_inc(sd_ready, 1)
                if live(s, 4):
                    q, u = (s // GROUP - 1) % 2, s % GROUP
                    if u == 0:
                        act.wait_ge(scale, g * NCHAIN)
                    act.activation(w1q(g - 1, 0, u), stage[:, q, u * 512:(u + 1) * 512], ACT.Copy, scale=kcol(g - 1, S1)).then_inc(whi_ready, 1)
                    act.activation(w2q(g - 1, 0, u), stage[:, q, W1N + u * 256:W1N + (u + 1) * 256], ACT.Copy, scale=kcol(g - 1, S2)).then_inc(whi_ready, 1)
            phase_a(act, step)

            act.wait_ge(blk, 12)
            act.wait_ge(scale, E * NCHAIN)

            def expert(eng, b):
                return eng.value_load(info[0:1, 0, bass.ds(b, 1)], min_val=0, max_val=E - 1)

            def front(b, k):
                e = expert(act, b)
                for f in range(HK):
                    act.wait_ge(h_ready, b * HK + f + 1)
                    if k >= 1:
                        act.wait_ge(prod_ready, (b - 1) * HK + f + 1)
                    act.activation(act1[:, f], bank[f][:, 0:BLOCK], ACT.Silu,
                                   bias=b1t[:, bass.ds(e, 1), f:f + 1].rearrange("p a f -> p (a f)"),
                                   scale=kcol(e, I1)).then_inc(act_ready, 1)
                act.wait_ge(g_in[k % 4], (b - k % 4) * 8 + 32)
                if k >= 2:
                    act.wait_ge(cw_ready, b - 1)
                act.activation(th[:, k % 2], G[:, k % 4, :, 2 * D:].bitcast(F32)[:, :, bass.ds(e, 1)].rearrange("p j a -> p (j a)"),
                               ACT.Tanh, scale=0.5).then_inc(th_ready, 1)
                act.wait_ge(prod_ready, (b + 1) * HK)
                if k >= 2:
                    act.wait_ge(y_ready, b - 1)
                act.activation(ab[:, k % 2, 0], prod[:, k % 2], ACT.Copy, scale=kcol(e, C2)).then_inc(ahi_ready, 1)
                act.wait_ge(th_ready, b + 1)
                if k >= 2:
                    act.wait_ge(y2_ready, (b - 1) * J)
                act.activation(cw[:, k % 2], th[:, k % 2], ACT.Copy, bias=0.5, scale=0.5).then_inc(cw_ready, 1)

            def back(b, k):
                act.wait_ge(y1_ready, b + 1)
                act.wait_ge(cw_ready, b + 1)
                if k >= 2:
                    act.wait_ge(added, (b - 1) * 32)
                for j in range(J):
                    act.activation(y2[:, k % 2, j], y1[:, k % 2, j], ACT.Copy, scale=cw[:, k % 2, j:j + 1]).then_inc(y2_ready, 1)
            phase_b(act, front, back)

        @block.vector
        def _(dve):
            dve.memset(eps[:], EPS).then_inc(const_dve, 1)
            dve.memset(Macc[:], 0.0)
            dve.memset(ones8[:], 1.0)
            dve.wait_ge(small_in, 16 * 8)
            dve.tensor_reduce(deg[:, 0], adj_n[:], AX.X, ALU.add).then_inc(const_dve, 1)
            dve.wait_ge(const_dve, 2)
            dve.tensor_scalar(deg[:, 1], deg[:, 0], 0.0, None, ALU.is_gt).then_inc(const_dve, 1)
            dve.tensor_scalar(deg[:, 2], deg[:, 0], 1e-37, None, ALU.max).then_inc(const_dve, 1)
            dve.tensor_copy(rw16[:, 0], rw[:]).then_inc(const_dve, 1)
            dve.wait_ge(const_dve, 5)
            dve.tensor_tensor(rw16[:, 1], rw[:], rw16[:, 0], ALU.subtract).then_inc(const_dve, 1)
            dve.wait_ge(deg_root, 1)
            dve.reciprocal(deg[:, 4], deg[:, 3]).then_inc(const_dve, 1)
            dve.wait_ge(const_dve, 7)
            dve.tensor_tensor(dinv[:], deg[:, 4], deg[:, 1], ALU.mult).then_inc(const_dve, 1)
            dve.wait_ge(const_dve, 8)
            for j in range(J):
                dve.tensor_scalar(At[:, j], At[:, j], dinv[:, j:j + 1], None, ALU.mult).then_inc(const_dve, 1)
            dve.wait_ge(const_pool, 10)
            dve.tensor_copy(rev[:], iota_i[:, 0]).then_inc(const_dve, 1)
            dve.tensor_scalar(pad_out[:], pad_ids, BLOCK - 1, TOKENS, ALU.bitwise_and, ALU.bitwise_or).then_inc(const_dve, 1)
            dve.tensor_copy(ebase[:], iota_i[:, 1]).then_inc(const_dve, 1)
            dve.tensor_copy(steps_f[:], steps_i[:]).then_inc(const_dve, 1)
            dve.wait_ge(const_dve, 14)

            def bc(ap):
                return ap.rearrange("p (t o) -> p t o", o=1).broadcast_to([P, TILES, E])

            def route_1(g, q):
                L, rt = lg[:, q], [0]
                n0 = g * NROUTE

                def go(ins):
                    ins.then_inc(route, 1)
                    rt[0] += 1
                    dve.wait_ge(route, n0 + rt[0])
                go(dve.tensor_reduce(m12[:, 0], L, AX.X, ALU.max))
                go(dve.tensor_tensor(ra[:, 0], L, bc(m12[:, 0]), ALU.is_equal))
                go(dve.tensor_tensor(ra[:, 0], ra[:, 0], rev[:], ALU.mult))
                go(dve.tensor_reduce(m12[:, 1], ra[:, 0], AX.X, ALU.max))
                go(dve.tensor_tensor(ra[:, 1], rev[:], bc(m12[:, 1]), ALU.is_equal))
                go(dve.scalar_tensor_tensor(ra[:, 2], ra[:, 1], -3e38, L, ALU.mult, ALU.add))
                go(dve.tensor_reduce(m12[:, 2], ra[:, 2], AX.X, ALU.max))
                go(dve.tensor_tensor(ra[:, 0], ra[:, 2], bc(m12[:, 2]), ALU.is_equal))
                go(dve.tensor_tensor(ra[:, 0], ra[:, 0], rev[:], ALU.mult))
                go(dve.tensor_reduce(m12[:, 3], ra[:, 0], AX.X, ALU.max))
                go(dve.tensor_tensor(ra[:, 3], rev[:], bc(m12[:, 3]), ALU.is_equal))
                go(dve.tensor_tensor(M[:, q], ra[:, 1], ra[:, 3], ALU.add))
                dve.tensor_tensor(m12[:, 4], m12[:, 0], m12[:, 2], ALU.subtract)
                go(dve.tensor_tensor(ra[:, 4], ra[:, 1], ra[:, 3], ALU.subtract))
                go(dve.tensor_tensor(xrow[:, q * GROUP:(q + 1) * GROUP, :, 2 * D:].bitcast(F32).rearrange("p b j e -> p (b j) e"),
                                     ra[:, 4], bc(m12[:, 4]), ALU.mult))

            def route_2(g, q):
                dve.wait_ge(rank_ready, g + 1)
                dve.tensor_reduce(Mg[:], M[:, q].rearrange("p t e -> p e t"), AX.X, ALU.add).then_inc(route, 1)
                dve.tensor_tensor(ra[:, 5], rkp, ebase[:], ALU.add).then_inc(route, 1)
                dve.wait_ge(route, g * NROUTE + 16)
                dve.tensor_tensor(Macc[:, 1 - q], Macc[:, q], Mg[:], ALU.add)
                dve.tensor_copy(gids[:, q], ids[:, bass.ds(g * TILES, TILES)])
                dve.tensor_tensor(ra[:, 1], ra[:, 1], ra[:, 5], ALU.mult)
                dve.tensor_tensor(ra[:, 3], ra[:, 3], ra[:, 5], ALU.mult).then_inc(route, 1)
                dve.wait_ge(route, g * NROUTE + 17)
                if True:
                    with nc.allow_low_precision("places are integers below 2**17, exact in float32"):
                        dve.tensor_reduce(slots[:, q, 0], ra[:, 1], AX.X, ALU.add)
                        dve.tensor_reduce(slots[:, q, 1], ra[:, 3], AX.X, ALU.add).then_inc(route, 1)

            def step(i, s, g):
                p, o = s % 2, 1 - s % 2
                if live(s, 1) or live(s, 3):
                    a, z = (0 if live(s, 1) else J), (2 * J if live(s, 3) else J)
                    dve.wait_ge(sd_ready, i)
                    dve.reciprocal(rs[:, o, a:z], sd[:, o, a:z]).then_inc(rs_ready, 1)
                if live(s, 0):
                    dve.wait_ge(x_in[s % 4], (i - s % 4) * 4 + 16)
                    for j in range(J):
                        dve.bn_stats(st[:, p, j], xin[:, s % 4, j]).then_inc(bn1, 1)
                if live(s, 1):
                    dve.wait_ge(rs_ready, i)
                    if s >= 3:
                        dve.wait_ge(t_ready, i - 2)
                    for j in range(J):
                        dve.tensor_scalar(xn1[:, o, j], xin[:, (s - 1) % 4, j], mv[:, o, j, 0:1], rs[:, o, j:j + 1],
                                          ALU.subtract, ALU.mult).then_inc(xn1_ready, 1)
                if live(s, 3):
                    dve.wait_ge(rs_ready, i)
                    if s >= 5:
                        dve.wait_ge(hi_ready, i - 4)
                    for j in range(J):
                        dve.tensor_scalar(xn2[:, o, j], x2[:, (s - 3) % 4, j], mv[:, o, J + j, 0:1], rs[:, o, J + j:J + j + 1],
                                          ALU.subtract, ALU.mult).then_inc(xn2_ready, 1)
                if live(s, 0):
                    hold(dve, bn1, (i + 1) * J)
                    for j in range(J):
                        dve.bn_aggr(mv[:, p, j], st[:, p, j]).then_inc(mv1, 1)
                if live(s, 2):
                    dve.wait_ge(g_ready, i - 1)
                    dve.wait_ge(xb_ready, i - 1)
                    if s >= 6:
                        dve.wait_ge(x2_stored[(s - 2) % 4], (i - 2 - (s - 2) % 4) * 4)
                    for j in range(J):
                        dve.scalar_tensor_tensor(x2[:, (s - 2) % 4, j], g_bank(s % 2)[:, j], dinv[:, j:j + 1],
                                                 xb[:, (s - 2) % 4, j], ALU.mult, ALU.add).then_inc(x2_ready, 1)
                    for j in range(J):
                        dve.wait_ge(x2_ready, (i - 2) * J + j + 1)
                        dve.bn_stats(st[:, p, J + j], x2[:, (s - 2) % 4, j]).then_inc(bn2, 1)
                    for j in range(J):
                        hold(dve, bn2, (i - 2) * J + j + 1)
                        dve.bn_aggr(mv[:, p, J + j], st[:, p, J + j]).then_inc(mv2, 1)
                if live(s, 3):
                    dve.wait_ge(hi_ready, i - 2)
                    dve.wait_ge(xn2_ready, (i - 2) * J)
                    if s - 3 >= 2 * GROUP and (s - 3) % GROUP == 0:
                        dve.wait_ge(row_stored[((s - 3) // GROUP) % 2], bufcount(i - 3, s - 3))
                    r = xrow[:, (s - 3) % 8]
                    dve.tensor_tensor(r[:, :, D:2 * D], xn2[:, o], r[:, :, 0:D], ALU.subtract).then_inc(lo_ready, 1)
                if live(s, 5):
                    c = (s - 5) % GROUP * J
                    dve.wait_ge(lgp_ready, i - 4)
                    dve.tensor_tensor(lg[:, ((s - 5) // GROUP) % 2, c:c + J], lgp,
                                      rb[:].rearrange("p (a e) -> p a e", a=1).broadcast_to([P, J, E]), ALU.add).then_inc(lg_ready, 1)
                if s % GROUP == 0 and live(s, 8):
                    dve.wait_ge(lg_ready, (g - 1) * GROUP)
                    route_1(g - 2, (s // GROUP) % 2)
                if s % GROUP == 1 and live(s, 9):
                    dve.wait_ge(scattered[(s // GROUP) % 2], parcount(g, s))
                    route_2(g - 2, (s // GROUP) % 2)
                if live(s, 0):
                    q, u = (s // GROUP) % 2, s % GROUP
                    if u == 0:
                        dve.wait_ge(w_in[q], (g - q) * 16 + 32)
                        if s >= 8:
                            dve.wait_ge(ar_ready, g - 1)
                        dve.tensor_reduce(am[:, q, 8:9], b1t[:, bass.ds(g, 1)].rearrange("p a f -> p (a f)"), AX.X, ALU.max,
                                          apply_absolute_value=True).then_inc(am_ready, 1)
                    dve.tensor_reduce(am[:, q, u:u + 1], stage[:, q, u * 512:(u + 1) * 512], AX.X, ALU.max,
                                      apply_absolute_value=True).then_inc(am_ready, 1)
                    dve.tensor_reduce(am[:, q, 4 + u:5 + u], stage[:, q, W1N + u * 256:W1N + (u + 1) * 256], AX.X, ALU.max,
                                      apply_absolute_value=True).then_inc(am_ready, 1)
                if live(s, 4):
                    q, u, e = (s // GROUP - 1) % 2, s % GROUP, g - 1
                    if u == 0:
                        scales(e, q)
                    dve.wait_ge(scale, g * NCHAIN)
                    for n, (dst, c, a, m) in enumerate(((w1q, S1, 0, 512), (w2q, S2, W1N, 256))):
                        dve.wait_ge(whi_ready, e * 8 + u * 2 + n + 1)
                        dve.scalar_tensor_tensor(dst(e, 1, u), stage[:, q, a + u * m:a + (u + 1) * m], kcol(e, c),
                                                 dst(e, 0, u), ALU.mult, ALU.subtract).then_inc(wlo_ready, 1)

            def parcount(g, s):
                q = (s // GROUP) % 2
                return (g - 2 - q) * (16 * 2 * TILES // 2) + 16

            def scales(e, q):
                n = [0]

                def go(ins):
                    ins.then_inc(scale, 1)
                    n[0] += 1
                    dve.wait_ge(scale, e * NCHAIN + n[0])
                dve.wait_ge(ar_ready, e + 1)
                dve.tensor_reduce(v[:, 2:3], ar[:, q, 4:8], AX.X, ALU.max)
                go(dve.tensor_reduce(v[:, 0:1], ar[:, q, 0:4], AX.X, ALU.max))
                go(dve.tensor_scalar(v[:, 1:2], v[:, 0:1], float(D), ar[:, q, 8:9], ALU.mult, ALU.add))
                go(dve.tensor_tensor(v[:, 1:2], v[:, 1:2], v[:, 1:2], ALU.mult))
                go(dve.tensor_scalar(v[:], v[:], 1e-30, None, ALU.max))
                go(dve.tensor_scalar(pw[:].bitcast(I32), v[:].bitcast(I32), 0x7F800000, None, ALU.bitwise_and))
                go(dve.reciprocal(rp[:], pw[:]))
                kk = K[:, bass.ds(e, 1)].rearrange("p a c -> p (a c)")
                go(dve.tensor_scalar(kk[:, S1:S1 + 1], rp[:, 0:1], TOP, None, ALU.mult))
                dve.tensor_scalar(kk[:, S2:S2 + 1], rp[:, 2:3], TOP, None, ALU.mult)
                go(dve.tensor_scalar(kk[:, I1:I1 + 1], pw[:, 0:1], 1.0 / TOP, None, ALU.mult))
                go(dve.tensor_tensor(kk[:, C2:C2 + 1], pw[:, 0:1], rp[:, 1:2], ALU.mult))
                go(dve.scalar_tensor_tensor(kk[:, CY:CY + 1], pw[:, 1:2], TOP ** -2, pw[:, 2:3], ALU.mult, ALU.mult))
                go(dve.tensor_scalar(beta[:, bass.ds(e, 1)].rearrange("p a f -> p (a f)"),
                                     b1t[:, bass.ds(e, 1), HK:].rearrange("p a f -> p (a f)"), kk[:, S1:S1 + 1], None, ALU.mult))
            phase_a(dve, step)

            n = [0]

            def go(ins):
                ins.then_inc(blk, 1)
                n[0] += 1
                dve.wait_ge(blk, n[0])

            def be(ap, m):
                return ap.rearrange("p (a e) -> p a e", a=1).broadcast_to([1, m, E])
            dve.wait_ge(tot_ready, 1)
            go(dve.tensor_copy(nb[:, 0], totp[0:1, :]))
            go(dve.tensor_tensor(cmp1, nb[:, 0].rearrange("p (e a) -> p e a", a=1).broadcast_to([1, E, 32]),
                                 steps_f[:, 0:32].rearrange("p (a s) -> p a s", a=1).broadcast_to([1, E, 32]), ALU.is_gt))
            go(dve.tensor_reduce(nb[:, 1], cmp1, AX.X, ALU.add))
            go(dve.tensor_tensor_scan(nb[:, 2], ones8[:], nb[:, 1], 0.0, ALU.mult, ALU.add))
            go(dve.tensor_tensor(cmp2[:, 0], steps_f[:, 32:].rearrange("p (b a) -> p b a", a=1).broadcast_to([1, MAX_BLOCKS, E]),
                                 be(nb[:, 2], MAX_BLOCKS), ALU.is_ge))
            go(dve.tensor_reduce(bl[:, 0], cmp2[:, 0], AX.X, ALU.add))
            go(dve.tensor_tensor(cmp2[:, 1], cmp2[:, 0], be(nb[:, 1], MAX_BLOCKS), ALU.mult))
            go(dve.tensor_reduce(bl[:, 1], cmp2[:, 1], AX.X, ALU.add))
            go(dve.tensor_tensor(bl[:, 2], steps_f[:, 32:], bl[:, 1], ALU.subtract))
            go(dve.scalar_tensor_tensor(info[:, 1, 0:MAX_BLOCKS], bl[:, 0], float(TOKENS // BLOCK), bl[:, 2], ALU.mult, ALU.add))
            dve.memset(info[:, 1, MAX_BLOCKS:], 0)
            dve.memset(info[:, 0, MAX_BLOCKS:], 0).then_inc(blk, 1)
            go(dve.tensor_scalar(info[:, 0, 0:MAX_BLOCKS], bl[:, 0], float(E - 1), None, ALU.min))

            def xt(b, k):
                dve.wait_ge(XTp_ready, b + 1)
                if k >= 2:
                    dve.wait_ge(h_ready, (b - 1) * HK)
                dve.tensor_copy(XT[:, k % 2], xTp).then_inc(XT_ready, 1)

            def front(b, k):
                e = dve.value_load(info[0:1, 0, bass.ds(b, 1)], min_val=0, max_val=E - 1)
                for f in range(HK):
                    dve.wait_ge(act_ready, b * HK + f + 1)
                    if k >= 2 and f == 0:
                        dve.wait_ge(ahi_ready, b - 1)
                        dve.wait_ge(alo_ready, b - 1)
                    dve.scalar_tensor_tensor(prod[:, k % 2, f], bank[f][:, BLOCK:], beta[:, bass.ds(e, 1), f:f + 1].rearrange("p a f -> p (a f)"),
                                             act1[:, f], ALU.add, ALU.mult).then_inc(prod_ready, 1)
                    if f == 1:
                        if isinstance(b, int) and b + 1 >= MAX_BLOCKS:
                            continue
                        xt(b + 1, k + 1)
                dve.wait_ge(ahi_ready, b + 1)
                dve.scalar_tensor_tensor(ab[:, k % 2, 1], prod[:, k % 2], kcol(e, C2), ab[:, k % 2, 0], ALU.mult, ALU.subtract).then_inc(alo_ready, 1)

            def back(b, k):
                e = dve.value_load(info[0:1, 0, bass.ds(b, 1)], min_val=0, max_val=E - 1)
                dve.wait_ge(y_ready, b + 1)
                if k >= 2:
                    dve.wait_ge(y2_ready, (b - 1) * J)
                dve.scalar_tensor_tensor(y1[:, k % 2], bank[5 + k % 2][:].rearrange("p (j d) -> p j d", j=J), kcol(e, CY),
                                         b2t[:, bass.ds(e, 1)].broadcast_to([P, J, D]), ALU.mult, ALU.add).then_inc(y1_ready, 1)
            xt(0, 0)
            phase_b(dve, front, back)

        @block.tensor
        def _(pe):
            def step(i, s, g):
                if s == 0:
                    pe.wait_ge(const_dve, 14)
                    pe.wait_ge(const_pool, 10)
                if s % GROUP == 1 and live(s, 9):
                    q = (s // GROUP) % 2
                    pe.wait_ge(route, (g - 2) * NROUTE + 12)
                    pe.matmul(rkp, tri[:], M[:, q], start=True, stop=False)
                    pe.matmul(rkp, ones[:], Macc[:, q].rearrange("p (a e) -> p a e", a=1).broadcast_to([P, TILES, E]), start=False, stop=False)
                    for c in range(TILES - 1):
                        mm = pe.matmul(rkp[:, c + 1:], ones[:], M[:, q, c:c + 1].broadcast_to([P, TILES - 1 - c, E]),
                                       start=False, stop=(c == TILES - 2))
                    mm.then_inc(rank_ready, 1)
                if live(s, 2):
                    pe.wait_ge(ts_ready, i - 1)
                    if s >= 4:
                        pe.wait_ge(x2_ready, (i - 3) * J)
                    for j in range(J):
                        for k in range(DK):
                            mm = pe.matmul(g_bank(s % 2)[:, j], ts[:, s % 2, k, j * P:(j + 1) * P], Wg[:, k], start=(k == 0), stop=(k == DK - 1))
                    mm.then_inc(g_ready, 1)
                if live(s, 4):
                    pe.wait_ge(lo_ready, i - 3)
                    pe.wait_ge(hi_ready, i - 3)
                    if s >= 5:
                        pe.wait_ge(xT_ready, i - 4)
                    for l in range(2):
                        for k in range(DK):
                            for j in range(J):
                                mm = pe.transpose(xTp[:, l, k, j * P:(j + 1) * P], xrow[:, (s - 4) % 8, j, l * D + k * P:l * D + (k + 1) * P], ident[:])
                    mm.then_inc(xTp_ready, 1)
                if live(s, 1):
                    pe.wait_ge(xn1_ready, i * J)
                    if s >= 3:
                        pe.wait_ge(ts_ready, i - 2)
                    for t in range(DK):
                        for m in range(J):
                            mm = pe.matmul(bank[(s - 1) % 2][:, t * NODES:(t + 1) * NODES], xn1[:, (s - 1) % 2, m, t * P:(t + 1) * P],
                                           At[:, m], start=(m == 0), stop=(m == J - 1))
                    mm.then_inc(t_ready, 1)
                if live(s, 5):
                    pe.wait_ge(xT_ready, i - 4)
                    if s >= 6:
                        pe.wait_ge(lg_ready, i - 5)
                    for j in range(J):
                        n = 0
                        for lx, lw in ((0, 0), (0, 1), (1, 0)):
                            for k in range(DK):
                                mm = pe.matmul(lgp[:, j], xT[:, (s - 5) % 2 ^ 0, lx, k, j * P:(j + 1) * P], rw16[:, lw, k], start=(n == 0), stop=(n == 5))
                                n += 1
                    mm.then_inc(lgp_ready, 1)
            phase_a(pe, step)
            pe.wait_ge(route, GROUPS * NROUTE)
            pe.matmul(totp, ones[:], Macc[:, GROUPS % 2], start=True, stop=True).then_inc(tot_ready, 1)

            pe.wait_ge(blk, 12)
            pe.wait_ge(wlo_ready, E * 8)
            pe.wait_ge(whi_ready, E * 8)

            def rows_t(b, k):
                pe.wait_ge(g_in[k % 4], (b - k % 4) * 8 + 32)
                if k >= 1:
                    pe.wait_ge(XT_ready, b)
                for l in range(2):
                    for c in range(DK):
                        for j in range(J):
                            mm = pe.transpose(xTp[:, l, c, j * P:(j + 1) * P], G[:, k % 4, j, l * D + c * P:l * D + (c + 1) * P], ident[:])
                mm.then_inc(XTp_ready, 1)

            def front(b, k):
                e = pe.value_load(info[0:1, 0, bass.ds(b, 1)], min_val=0, max_val=E - 1)
                pe.wait_ge(XT_ready, b + 1)
                for f in range(HK):
                    if k >= 1:
                        pe.wait_ge(prod_ready, (b - 1) * HK + f + 1)
                    for half in range(2):
                        n = 0
                        for c in range(DK):
                            for lw in range(2):
                                w = W1[:, bass.ds(e, 1), lw, c, half * H + f * P:half * H + (f + 1) * P].rearrange("p a n -> p (a n)")
                                for lx in range(2 - lw):
                                    mm = pe.matmul(bank[f][:, half * BLOCK:(half + 1) * BLOCK], w, XT[:, k % 2, lx, c], start=(n == 0), stop=(n == 5))
                                    n += 1
                    mm.then_inc(h_ready, 1)
                    if f == 1 and not (isinstance(b, int) and b + 1 >= MAX_BLOCKS):
                        rows_t(b + 1, k + 1)

            def back(b, k):
                e = pe.value_load(info[0:1, 0, bass.ds(b, 1)], min_val=0, max_val=E - 1)
                pe.wait_ge(ahi_ready, b + 1)
                pe.wait_ge(alo_ready, b + 1)
                if k >= 2:
                    pe.wait_ge(y1_ready, b - 1)
                n = 0
                for j in range(J):
                    n = 0
                    for c in range(HK):
                        for lw in range(2):
                            w = W2[:, bass.ds(e, 1), lw, c].rearrange("p a n -> p (a n)")
                            for la in range(2 - lw):
                                mm = pe.matmul(bank[5 + k % 2][:, j * D:(j + 1) * D], ab[:, k % 2, la, c, j * P:(j + 1) * P], w,
                                               start=(n == 0), stop=(n == 3 * HK - 1))
                                n += 1
                mm.then_inc(y_ready, 1)
            rows_t(0, 0)
            phase_b(pe, front, back)


def kernel(x, adj, L0_gnn_weight, L0_gnn_bias, L0_ffn_router_w, L0_ffn_router_b, L0_ffn_fc1_w, L0_ffn_fc1_b,
           L0_ffn_fc2_w, L0_ffn_fc2_b):
    import numpy as np
    import concourse.bacc as bacc
    from concourse.bass_utils import run_bass_kernel_spmd

    def tiles(a):
        a = np.asarray(a)
        return np.ascontiguousarray(a.reshape(a.shape[0] // P, P, a.shape[1]).transpose(1, 0, 2))

    fc1 = np.asarray(L0_ffn_fc1_w)
    fc2 = np.asarray(L0_ffn_fc2_w)
    arrays = {
        "x": np.ascontiguousarray(np.asarray(x).reshape(TOKENS, D)),
        "adj": tiles(adj),
        "adj_t": tiles(np.asarray(adj).T),
        "gnn_w": tiles(L0_gnn_weight),
        "gnn_b": np.asarray(L0_gnn_bias),
        "router_w": tiles(np.asarray(L0_ffn_router_w).T),
        "router_b": np.asarray(L0_ffn_router_b),
        "w1": np.ascontiguousarray(fc1.reshape(E, 2 * H, DK, P).transpose(0, 3, 2, 1).reshape(E, P, W1N)),
        "b1": np.ascontiguousarray(np.asarray(L0_ffn_fc1_b).reshape(E, FT, P).transpose(2, 0, 1)),
        "w2": np.ascontiguousarray(fc2.reshape(E, D, HK, P).transpose(0, 3, 2, 1).reshape(E, P, W2N)),
        "b2": np.asarray(L0_ffn_fc2_b),
    }
    nc = bacc.Bacc("TRN2", target_bir_lowering=False, num_devices=1)
    feed, args = {}, []
    for name, a in arrays.items():
        feed[f"in_{name}"] = a
        args.append(nc.dram_tensor(f"in_{name}", a.shape, mybir.dt.from_np(a.dtype), kind="ExternalInput").ap())
    out = nc.dram_tensor("out", (TOKENS + BLOCK, D), F32, kind="ExternalOutput").ap()
    program(nc, *args, out)
    r = run_bass_kernel_spmd(nc, [feed], core_ids=[0])
    return r.results[0]["out"][:TOKENS].reshape(BATCHES, NODES, D)
```

```python
from contextlib import ExitStack

import concourse.bass as bass
from concourse import mybir

F32 = mybir.dt.float32
F16 = mybir.dt.float16
BF16 = mybir.dt.bfloat16
I32 = mybir.dt.int32
ALU = mybir.AluOpType
ACT = mybir.ActivationFunctionType
AX = mybir.AxisListType

P = 128
D = 256
DK = D // P
BATCHES = 32
NODES = 256
J = NODES // P
TOKENS = BATCHES * NODES
E = 8
H = 512
HK = H // P
FT = 2 * H // P
BLOCK = 256
MAX_BLOCKS = (2 * TOKENS + E * (BLOCK - 1)) // BLOCK
GROUP = 4
TILES = GROUP * J
GROUPS = BATCHES // GROUP
TABLE = E * TOKENS + MAX_BLOCKS * BLOCK
ROW = 2 * D + 2 * E
W1N = DK * 2 * H
W2N = HK * D
EPS = 1e-5
TOP = 2.0 ** 14
S1, I1, C2, S2, CY = range(5)

IDX_RING = 8
AHEAD = 3
CONST_DVE = 9
NCHAIN = 8
NROUTE = 18


def program(nc, x, adj, adj_t, gnn_w, gnn_b, router_w, router_b, w1, b1, w2, b2, out):
    x_v = x.rearrange("(b j p) d -> b p j d", j=J, p=P)
    out_v = out.rearrange("(b j p) d -> b p j d", j=J, p=P)
    rows = nc.dram_tensor("rows", (TOKENS + BLOCK, ROW // 2), I32, kind="Internal").ap()
    rows_v = rows.rearrange("(g t p) c -> g p t c", t=2, p=P)
    table = nc.dram_tensor("table", (TABLE, 1), I32, kind="Internal").ap()
    table_b = table.rearrange("(b p j) o -> b p (j o)", p=P, j=2)

    with ExitStack() as ctx:
        def sb(name, shape, dt=F32):
            return ctx.enter_context(nc.sbuf_tensor(name, shape, dt))

        def sem(name):
            return ctx.enter_context(nc.semaphore(name))

        bank = [ctx.enter_context(nc.psum_tensor(f"bank{i}", [P, 512], F32)) for i in range(8)]

        W1 = sb("W1", [P, E, 2, DK, 2 * H], F16)
        W2 = sb("W2", [P, E, 2, HK, D], F16)
        stage = sb("stage", [P, 2, W1N + W2N])
        ident = sb("ident", [P, P], F16)
        tri = sb("tri", [P, P], F16)
        ones = sb("ones", [P, P], F16)
        ones_b = sb("ones_b", [P, P], BF16)
        ones_f = sb("ones_f", [P, P])
        eps = sb("eps", [P, 1])
        ids = sb("ids", [P, BATCHES * J], I32)
        iota_i = sb("iota_i", [P, 2, TILES, E], I32)
        rev = sb("rev", [P, TILES, E])
        ebase = sb("ebase", [P, TILES, E])
        steps_i = sb("steps_i", [1, 32 + MAX_BLOCKS], I32)
        steps_f = sb("steps_f", [1, 32 + MAX_BLOCKS])
        pad_out = sb("pad_out", [P, TABLE // P], I32)
        zeros = sb("zeros", [P, 2, ROW // 2], I32)
        ones8 = sb("ones8", [1, E])
        adj_n = sb("adj_n", [P, J, NODES])
        At = sb("At", [P, J, NODES])
        Wg = sb("Wg", [P, DK, D])
        bg = sb("bg", [P, D])
        rw = sb("rw", [P, DK, E])
        rw16 = sb("rw16", [P, 2, DK, E], F16)
        rb = sb("rb", [P, E])
        b1t = sb("b1t", [P, E, FT])
        b2t = sb("b2t", [P, E, D])
        deg = sb("deg", [P, 2, J + NODES])
        bias_rest = sb("bias_rest", [P, D])
        bias_part = sb("bias_part", [P, 3, D], BF16)
        bias_rows = sb("bias_rows", [P, D], BF16)
        xin = sb("xin", [P, 4, J, D])
        st = sb("st", [P, 2, 2 * J, 6])
        mv = sb("mv", [P, 2, 2 * J, 2])
        sd = sb("sd", [P, 2, 2 * J])
        rs = sb("rs", [P, 2, 2 * J])
        nmr = sb("nmr", [P, 2, 2 * J])
        xn1 = sb("xn1", [P, 2, J, D])
        ts = sb("ts", [P, 2, DK, NODES])
        x2 = sb("x2", [P, 4, J, D])
        xn2 = sb("xn2", [P, 2, J, D])
        xrow = sb("xrow", [P, 2 * GROUP, J, ROW], F16)
        xT = sb("xT", [P, 2, 2, DK, NODES], F16)
        pad_ids = xT[:].rearrange("p a l k n -> p (a l k n)").bitcast(I32)[:, 0:TABLE // P]
        lg = sb("lg", [P, 2, TILES, E])
        m12 = sb("m12", [P, 5, TILES])
        ra = sb("ra", [P, 6, TILES, E])
        M = sb("M", [P, 2, TILES, E], F16)
        Mg = sb("Mg", [P, E])
        Macc = sb("Macc", [P, 2, E], F16)
        gids = sb("gids", [P, 2, TILES], I32)
        slots = sb("slots", [P, 2, 2, TILES], I32)
        am = sb("am", [P, 2, 5])
        ar = sb("ar", [P, 2, 5])
        junk = sb("junk", [P, W2N // 2], BF16)
        v = sb("v", [P, 3])
        pw = sb("pw", [P, 3])
        rp = sb("rp", [P, 3])
        K = sb("K", [P, E, 5])
        beta = sb("beta", [P, E, HK])
        nb = sb("nb", [1, 4, E])
        spare = xin[0:1].rearrange("p a j d -> p (a j d)")
        cmp1 = spare[:, 1536:1536 + 32 * E].rearrange("p (e s) -> p e s", e=E)
        cmp2 = spare[:, 0:2 * MAX_BLOCKS * E].rearrange("p (a b e) -> p a b e", a=2, e=E)
        bl = sb("bl", [1, 4, MAX_BLOCKS])
        info = sb("info", [1, 2, MAX_BLOCKS + 1], I32)
        idx = sb("idx", [P, IDX_RING, 2], I32)
        G = xrow[:, 0:4]
        XT = xn1[:].rearrange("p a j d -> p (a j d)").bitcast(F16).rearrange("p (a l k n) -> p a l k n", a=2, l=2, k=DK)
        free = stage[:].rearrange("p a n -> p (a n)")
        N = HK * BLOCK
        act1 = free[:, 0:N].rearrange("p (f n) -> p f n", f=HK)
        prod = free[:, N:3 * N].rearrange("p (a f n) -> p a f n", a=2, f=HK)
        ab = free[:, 3 * N:5 * N].bitcast(F16).rearrange("p (a l f n) -> p a l f n", a=2, l=2, f=HK)
        th = sb("th", [P, 2, 2])
        cw = sb("cw", [P, 2, 2])
        y1 = xin[:, 2:4]
        y2 = x2[:, 0:2]

        def g_bank(b2):
            return bank[2 + b2][:].rearrange("p (j d) -> p j d", j=J)

        xTp = bank[4][:].bitcast(F16).rearrange("p (l k n) -> p l k n", l=2, k=DK)
        lgp = bank[5][:, 0:J * E].rearrange("p (j e) -> p j e", j=J)
        rkp = bank[6][:, 0:TILES * E].rearrange("p (t e) -> p t e", t=TILES)
        totp = bank[7][:, 0:E]
        b1v = b1t[:]

        small_in = sem("small_in")
        x_in = [sem(f"x_in{i}") for i in range(4)]
        w_in = [sem(f"w_in{i}") for i in range(2)]
        const_pool = sem("const_pool")
        const_dve = sem("const_dve")
        pad_out_ready = sem("pad_out_ready")
        deg_root = sem("deg_root")
        pad_stored = sem("pad_stored")
        degree_ready = sem("degree_ready")
        bn1 = sem("bn1")
        bn2 = sem("bn2")
        mv1 = sem("mv1")
        mv2 = sem("mv2")
        sd_ready = sem("sd_ready")
        rs_ready = sem("rs_ready")
        nmr_ready = sem("nmr_ready")
        xn1_ready = sem("xn1_ready")
        t_ready = sem("t_ready")
        ts_ready = sem("ts_ready")
        g_ready = sem("g_ready")
        x2_ready = sem("x2_ready")
        x2_stored = [sem(f"x2_stored{i}") for i in range(4)]
        xn2_ready = sem("xn2_ready")
        hi_ready = sem("hi_ready")
        lo_ready = sem("lo_ready")
        xTp_ready = sem("xTp_ready")
        xT_ready = sem("xT_ready")
        lgp_ready = sem("lgp_ready")
        lg_ready = sem("lg_ready")
        route = sem("route")
        rank_ready = sem("rank_ready")
        row_stored = [sem(f"row_stored{i}") for i in range(2)]
        scattered = [sem(f"scattered{i}") for i in range(2)]
        am_ready = sem("am_ready")
        sum_ready = sem("sum_ready")
        ar_ready = sem("ar_ready")
        scale = sem("scale")
        whi_ready = sem("whi_ready")
        wlo_ready = sem("wlo_ready")
        tot_ready = sem("tot_ready")
        blk = sem("blk")
        idx_in = [sem(f"idx_in{i}") for i in range(IDX_RING)]
        g_in = [sem(f"g_in{i}") for i in range(4)]
        XTp_ready = sem("XTp_ready")
        XT_ready = sem("XT_ready")
        h_ready = sem("h_ready")
        act_ready = sem("act_ready")
        prod_ready = sem("prod_ready")
        ahi_ready = sem("ahi_ready")
        alo_ready = sem("alo_ready")
        y_ready = sem("y_ready")
        y1_ready = sem("y1_ready")
        th_ready = sem("th_ready")
        cw_ready = sem("cw_ready")
        y2_ready = sem("y2_ready")
        added = sem("added")

        block = ctx.enter_context(nc.Block())

        LAST = BATCHES + 2 * GROUP // 2 + 2

        def phase_a(eng, step):
            for i in range(8):
                step(i, i, i // GROUP)
            with eng.Fori(8 // GROUP, GROUPS - 1, 2) as g0:
                for u in range(8):
                    step(g0 * GROUP + u, 8 + u, g0 + u // GROUP)
            for i in range(BATCHES, LAST):
                step(i, i, i // GROUP)

        def live(s, back, n=BATCHES):
            return back <= s < n + back

        def hold(eng, sem, value):
            if not isinstance(value, int):
                value = eng.to_reg(value)
                eng.wait_ge(sem, 1)
            eng.wait_ge(sem, value)

        def bufcount(b, s):
            if isinstance(b, int):
                return 16 * ((b // GROUP) // 2)
            return (b - (s % 8)) * 2

        def kcol(e, c):
            return K[:, bass.ds(e, 1), c:c + 1].rearrange("p a c -> p (a c)")

        def w1_half(e, part, u):
            return W1[:].rearrange("p e l k f -> p e l (k f)")[:, bass.ds(e, 1), part, u * W1N // 2:(u + 1) * W1N // 2].rearrange("p a n -> p (a n)")

        def w2_half(e, part, u):
            return W2[:].rearrange("p e l k f -> p e l (k f)")[:, bass.ds(e, 1), part, u * W2N // 2:(u + 1) * W2N // 2].rearrange("p a n -> p (a n)")

        def phase_b(eng, front, back):
            front(0, 0)
            n = 4
            for b in range(1, n):
                front(b, b)
                back(b - 1, b - 1)
            with eng.Fori(n, (MAX_BLOCKS - n) // 4 * 4 + 1, 4) as b0:
                for k in range(4):
                    front(b0 + k, n + k)
                    back(b0 + k - 1, n + k - 1)
            for b in range(n + (MAX_BLOCKS - n) // 4 * 4, MAX_BLOCKS):
                front(b, b)
                back(b - 1, b - 1)
            back(MAX_BLOCKS - 1, MAX_BLOCKS - 1)

        @block.sync
        def _(sp):
            for dst, src in ((adj_n, adj), (At, adj_t), (Wg, gnn_w), (rw, router_w), (b1t, b1)):
                sp.dma_start(dst[:], src).then_inc(small_in, 16)
            sp.dma_start(bg[:], gnn_b.rearrange("(a d) -> a d", a=1).broadcast_to([P, D])).then_inc(small_in, 16)
            sp.dma_start(rb[:], router_b.rearrange("(a d) -> a d", a=1).broadcast_to([P, E])).then_inc(small_in, 16)
            sp.dma_start(b2t[:], b2.rearrange("(a e) d -> a e d", a=1).broadcast_to([P, E, D])).then_inc(small_in, 16)

            def load_w(g, q, u):
                for src, a, n in ((w1, 0, W1N // 2), (w2, W1N, W2N // 2)):
                    sp.dma_start(stage[:, q, a + u * n:a + (u + 1) * n],
                                 src[bass.ds(g, 1), :, u * n:(u + 1) * n].rearrange("a p n -> p (a n)")).then_inc(w_in[q], 16)

            def step(i, s, g):
                if live(s, 0):
                    if s >= 4:
                        hold(sp, x2_ready, i - 3)
                    sp.dma_start(xin[:, s % 4], x_v[bass.ds(i, 1)].rearrange("a p j d -> p (a j) d")).then_inc(x_in[s % 4], 16)
                if s % GROUP < 2 and live(s, 0):
                    u = s % GROUP
                    if s >= 2 * GROUP:
                        sp.wait_ge(whi_ready, (g - 2) * 4 + 2 * u + 2)
                        hold(sp, wlo_ready, (g - 2) * 4 + 2 * u + 2)
                    load_w(g, (s // GROUP) % 2, u)
                if live(s, 3):
                    hold(sp, x2_ready, i - 2)
                    sp.dma_start(out_v[bass.ds(i - 3, 1)].rearrange("a p j d -> p (a j) d"), x2[:, (s - 3) % 4]).then_inc(x2_stored[(s - 3) % 4], 16)
                if s % GROUP == 1 and live(s, 9):
                    hold(sp, route, (g - 2) * NROUTE + 14)
                    hold(sp, lo_ready, (g - 1) * GROUP)
                    q = (s // GROUP) % 2
                    sp.dma_start(rows_v[bass.ds((g - 2) * GROUP, GROUP)].rearrange("b p j c -> p b j c"),
                                 xrow[:, q * GROUP:(q + 1) * GROUP].bitcast(I32)).then_inc(row_stored[q], 16)
            sp.wait_ge(const_pool, 10)
            sp.dma_start(rows_v[BATCHES], zeros[:]).then_inc(pad_stored, 16)
            sp.dma_start(out_v[BATCHES], zeros[:, :, 0:D].bitcast(F32)).then_inc(pad_stored, 16)
            phase_a(sp, step)

            for s in scattered:
                sp.wait_ge(s, 16 + 16 * 2 * TILES * GROUPS // 2)
            sp.wait_ge(blk, 12)

            def load_idx(b, k):
                start = sp.value_load(info[0:1, 1, bass.ds(b, 1)], min_val=0, max_val=TABLE // BLOCK - 1)
                sp.dma_start(idx[:, k], table_b[bass.ds(start, 1)].rearrange("a p j -> p (a j)")).then_inc(idx_in[k], 16)

            for b in range(IDX_RING):
                load_idx(b, b)
            full = MAX_BLOCKS // IDX_RING * IDX_RING
            with sp.Fori(IDX_RING, full, IDX_RING) as b0:
                for k in range(IDX_RING):
                    hold(sp, added, (b0 + k - IDX_RING + 1) * 32)
                    load_idx(b0 + k, k)
            for b in range(full, MAX_BLOCKS):
                sp.wait_ge(added, (b - IDX_RING + 1) * 32)
                load_idx(b, b % IDX_RING)
            sp.wait_ge(added, MAX_BLOCKS * 32)

        @block.gpsimd
        def _(pool):
            pool.memset(zeros[:], 0).then_inc(const_pool, 1)
            pool.memset(ones[:], 1.0).then_inc(const_pool, 1)
            pool.memset(ones_f[:], 1.0).then_inc(const_pool, 1)
            pool.memset(ones_b[:], 1.0).then_inc(const_pool, 1)
            pool.iota(pad_ids, pattern=[[1, TABLE // P]], base=0, channel_multiplier=TABLE // P).then_inc(const_pool, 1)
            pool.iota(ids[:], pattern=[[P, BATCHES * J]], base=0, channel_multiplier=1).then_inc(const_pool, 1)
            pool.iota(iota_i[:, 0], pattern=[[0, TILES], [-1, E]], base=E, channel_multiplier=0).then_inc(const_pool, 1)
            pool.iota(iota_i[:, 1], pattern=[[0, TILES], [TOKENS, E]], base=0, channel_multiplier=0).then_inc(const_pool, 1)
            pool.iota(steps_i[:, 0:32], pattern=[[BLOCK, 32]], base=0, channel_multiplier=0).then_inc(const_pool, 1)
            pool.iota(steps_i[:, 32:], pattern=[[1, MAX_BLOCKS]], base=0, channel_multiplier=0).then_inc(const_pool, 1)
            pool.wait_ge(const_pool, 10)
            pool.affine_select(out=tri[:], in_=ones[:], pattern=[[1, P]], compare_op=ALU.is_gt, fill=0.0,
                               base=0, channel_multiplier=-1).then_inc(const_pool, 1)
            pool.affine_select(out=ident[:], in_=ones[:], pattern=[[1, P]], compare_op=ALU.is_equal, fill=0.0,
                               base=0, channel_multiplier=-1).then_inc(const_pool, 1)
            pool.wait_ge(pad_out_ready, 1)
            half = TABLE // P // 2
            for q in range(2):
                pool.dma_start(table.rearrange("(p c) o -> p (c o)", p=P)[:, q * half:(q + 1) * half],
                             pad_out[:, q * half:(q + 1) * half]).then_inc(scattered[q], 16)
            for q in scattered:
                pool.wait_ge(q, 16)

            def scatter(i, s, g, c):
                q = (s // GROUP) % 2
                for k in range(2):
                    pool.indirect_dma_start(
                        table, bass.IndirectOffsetOnAxis(ap=slots[:, q, k, c:c + 1], axis=0),
                        gids[:, q, c:c + 1], None).then_inc(scattered[q], 16)

            def step(i, s, g):
                if s % GROUP == 3 and live(s, 0):
                    hold(pool, am_ready, (g + 1) * 3)
                    hold(pool, sum_ready, (g + 1) * 2)
                    q = (s // GROUP) % 2
                    pool.partition_all_reduce(ar[:, q], am[:, q], P, bass.bass_isa.ReduceOp.max).then_inc(ar_ready, 1)
                if s % GROUP in (2, 3) and live(s - s % GROUP, 8):
                    if s % GROUP == 2:
                        hold(pool, route, (g - 1) * NROUTE)
                    for c in range((s % GROUP - 2) * 4, (s % GROUP - 1) * 4):
                        scatter(i, s, g - 2, c)
            phase_a(pool, step)
            pool.wait_ge(route, GROUPS * NROUTE)
            for c in range(TILES if LAST % GROUP <= 2 else 0):
                scatter(LAST, (GROUPS + 1) * GROUP, GROUPS - 1, c)

            pool.wait_ge(pad_stored, 16 * 2)
            for s in row_stored:
                pool.wait_ge(s, 16 * GROUPS // 2)
            for s in x2_stored:
                pool.wait_ge(s, 16 * BATCHES // 4)

            def gather(b, k):
                hold(pool, idx_in[k % IDX_RING], (b - k % IDX_RING) * 2 + 16)
                if k >= 4:
                    hold(pool, XTp_ready, b - 3)
                    pool.wait_ge(th_ready, b - 3)
                for j in range(J):
                    pool.indirect_dma_start(G[:, k % 4, j].bitcast(I32), None, rows,
                                            bass.IndirectOffsetOnAxis(ap=idx[:, k % IDX_RING, j:j + 1], axis=0)).then_inc(g_in[k % 4], 16)

            def add(b, k):
                pool.wait_ge(y2_ready, (b + 1) * J)
                if k >= 1:
                    hold(pool, added, b * 32)
                for j in range(J):
                    pool.indirect_dma_start(out, bass.IndirectOffsetOnAxis(ap=idx[:, k % IDX_RING, j:j + 1], axis=0),
                                            y2[:, k % 2, j], None, compute_op=ALU.add).then_inc(added, 16)

            for b in range(AHEAD + 1):
                gather(b, b)
            add(0, 0)
            first = AHEAD + 1
            full = (MAX_BLOCKS - first) // IDX_RING * IDX_RING + first
            with pool.Fori(first, full, IDX_RING) as b0:
                for k in range(IDX_RING):
                    gather(b0 + k, first + k)
                    add(b0 + k - AHEAD, first + k - AHEAD)
            for b in range(full, MAX_BLOCKS):
                gather(b, b)
                add(b - AHEAD, b - AHEAD)
            for b in range(MAX_BLOCKS - AHEAD, MAX_BLOCKS):
                add(b, b)

        @block.scalar
        def _(act):
            act.wait_ge(const_dve, 3)
            act.activation(deg[:, 0], deg[:, 0], ACT.Sqrt).then_inc(deg_root, 1)

            def step(i, s, g):
                p, o = s % 2, 1 - s % 2
                if live(s, 1):
                    act.wait_ge(nmr_ready, i)
                    if s >= 3:
                        act.wait_ge(t_ready, i - 2)
                    for j in range(J):
                        act.activation(xn1[:, o, j], xin[:, (s - 1) % 4, j], ACT.Identity, bias=nmr[:, o, j:j + 1],
                                       scale=rs[:, o, j:j + 1]).then_inc(xn1_ready, 1)
                if live(s, 3):
                    act.wait_ge(nmr_ready, i)
                    if s >= 5:
                        act.wait_ge(lo_ready, i - 4)
                    for j in range(J):
                        act.activation(xn2[:, o, j], x2[:, (s - 3) % 4, j], ACT.Identity, bias=nmr[:, o, J + j:J + j + 1],
                                       scale=rs[:, o, J + j:J + j + 1]).then_inc(xn2_ready, 1)
                    act.wait_ge(xn2_ready, (i - 2) * J)
                    if s - 3 >= 2 * GROUP and (s - 3) % GROUP == 0:
                        act.wait_ge(row_stored[((s - 3) // GROUP) % 2], bufcount(i - 3, s - 3))
                    act.activation(xrow[:, (s - 3) % 8, :, 0:D], xn2[:, (s - 3) % 2], ACT.Copy).then_inc(hi_ready, 1)
                if live(s, 4):
                    act.wait_ge(xTp_ready, i - 3)
                    if s >= 6:
                        act.wait_ge(lgp_ready, i - 5)
                    act.activation(xT[:, s % 2], xTp, ACT.Copy).then_inc(xT_ready, 1)
                if live(s, 0) or live(s, 2):
                    a, z = (0 if live(s, 0) else J), (2 * J if live(s, 2) else J)
                    if live(s, 0):
                        act.wait_ge(mv1, (i + 1) * J)
                    if live(s, 2):
                        act.wait_ge(mv2, (i - 1) * J)
                    if s == 0:
                        act.wait_ge(const_dve, 1)
                    if s >= 2:
                        act.wait_ge(rs_ready, i - 1)
                    act.activation(sd[:, p, a:z], mv[:, p, a:z, 1], ACT.Sqrt, bias=eps[:]).then_inc(sd_ready, 1)
                if live(s, 1):
                    act.wait_ge(t_ready, i)
                    if s >= 3:
                        act.wait_ge(g_ready, i - 2)
                    act.activation(ts[:, (s - 1) % 2], bank[(s - 1) % 2][:].rearrange("p (k n) -> p k n", k=DK), ACT.Copy).then_inc(ts_ready, 1)
                if s % GROUP in (1, 2) and live(s - s % GROUP, 4):
                    q, u, e = (s // GROUP - 1) % 2, s % GROUP - 1, g - 1
                    act.wait_ge(scale, g * NCHAIN)
                    for dst, c, a, n in ((w1_half, S1, 0, W1N // 2), (w2_half, S2, W1N, W2N // 2)):
                        act.activation(dst(e, 0, u), stage[:, q, a + u * n:a + (u + 1) * n], ACT.Copy, scale=kcol(e, c)).then_inc(whi_ready, 1)
                if live(s, 0) and s % GROUP >= 2:
                    q, u = (s // GROUP) % 2, s % GROUP - 2
                    act.wait_ge(w_in[q], (g - q) * 32 + 32 * (u + 1))
                    if u == 0 and s >= 8:
                        act.wait_ge(ar_ready, g - 1)
                    act.activation(junk[:], stage[:, q, W1N + u * 512:W1N + (u + 1) * 512], ACT.Abs,
                                   accum_out=am[:, q, 2 + u:3 + u]).then_inc(sum_ready, 1)
            phase_a(act, step)

            act.wait_ge(blk, 12)
            act.wait_ge(scale, E * NCHAIN)

            def expert(eng, b):
                return eng.value_load(info[0:1, 0, bass.ds(b, 1)], min_val=0, max_val=E - 1)

            def front(b, k):
                e = expert(act, b)
                for f in range(HK):
                    act.wait_ge(h_ready, b * HK + f + 1)
                    if k >= 1:
                        act.wait_ge(prod_ready, (b - 1) * HK + f + 1)
                    act.activation(act1[:, f], bank[f][:, 0:BLOCK], ACT.Silu,
                                   bias=b1t[:, bass.ds(e, 1), f:f + 1].rearrange("p a f -> p (a f)"),
                                   scale=kcol(e, I1)).then_inc(act_ready, 1)
                act.wait_ge(g_in[k % 4], (b - k % 4) * 8 + 32)
                if k >= 2:
                    act.wait_ge(cw_ready, b - 1)
                act.activation(th[:, k % 2], G[:, k % 4, :, 2 * D:].bitcast(F32)[:, :, bass.ds(e, 1)].rearrange("p j a -> p (j a)"),
                               ACT.Tanh, scale=0.5).then_inc(th_ready, 1)
                act.wait_ge(prod_ready, (b + 1) * HK)
                if k >= 2:
                    act.wait_ge(y_ready, b - 1)
                act.activation(ab[:, k % 2, 0], prod[:, k % 2], ACT.Copy, scale=kcol(e, C2)).then_inc(ahi_ready, 1)
                act.wait_ge(th_ready, b + 1)
                if k >= 2:
                    act.wait_ge(y2_ready, (b - 1) * J)
                act.activation(cw[:, k % 2], th[:, k % 2], ACT.Copy, bias=0.5, scale=0.5).then_inc(cw_ready, 1)

            def back(b, k):
                act.wait_ge(y1_ready, b + 1)
                act.wait_ge(cw_ready, b + 1)
                if k >= 2:
                    act.wait_ge(added, (b - 1) * 32)
                for j in range(J):
                    act.activation(y2[:, k % 2, j], y1[:, k % 2, j], ACT.Copy, scale=cw[:, k % 2, j:j + 1]).then_inc(y2_ready, 1)
            phase_b(act, front, back)

        @block.vector
        def _(dve):
            n = [0]

            def put(ins):
                ins.then_inc(const_dve, 1)
                n[0] += 1
                dve.wait_ge(const_dve, n[0])
            put(dve.memset(eps[:], EPS))
            dve.memset(Macc[:], 0.0)
            dve.memset(ones8[:], 1.0)
            dve.memset(bias_rows[:], 0.0)
            dve.wait_ge(small_in, 16 * 8)
            dve.tensor_reduce(deg[:, 0, 0:J], adj_n[:], AX.X, ALU.add)
            dve.wait_ge(degree_ready, 1)
            put(dve.tensor_copy(deg[:, 0, J:], bank[7][:, 0:NODES]))
            dve.tensor_scalar(deg[:, 1], deg[:, 0], 0.0, None, ALU.is_gt)
            put(dve.tensor_scalar(deg[:, 0], deg[:, 0], 1e-37, None, ALU.max))
            dve.tensor_copy(bias_part[:, 0], bg[:])
            put(dve.tensor_copy(rw16[:, 0], rw[:]))
            dve.tensor_tensor(rw16[:, 1], rw[:], rw16[:, 0], ALU.subtract)
            put(dve.tensor_tensor(bias_rest[:], bg[:], bias_part[:, 0], ALU.subtract))
            put(dve.tensor_copy(bias_part[:, 1], bias_rest[:]))
            put(dve.tensor_tensor(bias_part[:, 2], bias_rest[:], bias_part[:, 1], ALU.subtract))
            for k in range(3):
                dve.tensor_copy(bias_rows[32 * k:32 * k + 1], bias_part[32 * k:32 * k + 1, k])
            dve.wait_ge(deg_root, 1)
            put(dve.reciprocal(deg[:, 0], deg[:, 0]))
            put(dve.tensor_tensor(deg[:, 0], deg[:, 0], deg[:, 1], ALU.mult))
            for j in range(J):
                dve.scalar_tensor_tensor(At[:, j], At[:, j], deg[:, 0, j:j + 1], deg[:, 0, J:], ALU.mult, ALU.mult)
            dve.wait_ge(const_pool, 12)
            dve.tensor_copy(rev[:], iota_i[:, 0])
            dve.tensor_scalar(pad_out[:], pad_ids, BLOCK - 1, TOKENS, ALU.bitwise_and, ALU.bitwise_or).then_inc(pad_out_ready, 1)
            dve.tensor_copy(ebase[:], iota_i[:, 1])
            put(dve.tensor_copy(steps_f[:], steps_i[:]))

            def bc(ap):
                return ap.rearrange("p (t o) -> p t o", o=1).broadcast_to([P, TILES, E])

            def route_and_scales(g, q, e, x):
                r, z = g is not None, e is not None

                def routed(k):
                    dve.wait_ge(route, g * NROUTE + k)

                def scaled(k):
                    dve.wait_ge(scale, e * NCHAIN + k)
                L = lg[:, q]
                if r:
                    dve.tensor_reduce(m12[:, 0], L, AX.X, ALU.max).then_inc(route, 1)
                if z:
                    kk = K[:, bass.ds(e, 1)].rearrange("p a c -> p (a c)")
                    dve.wait_ge(ar_ready, e + 1)
                    dve.tensor_reduce(v[:, 2:3], ar[:, x, 2:4], AX.X, ALU.max)
                    dve.tensor_reduce(v[:, 0:1], ar[:, x, 0:2], AX.X, ALU.max).then_inc(scale, 1)
                if r:
                    routed(1)
                    dve.tensor_tensor(ra[:, 0], L, bc(m12[:, 0]), ALU.is_equal).then_inc(route, 1)
                if z:
                    scaled(1)
                    dve.tensor_scalar(v[:, 1:2], v[:, 0:1], float(D), ar[:, x, 4:5], ALU.mult, ALU.add).then_inc(scale, 1)
                if r:
                    routed(2)
                    dve.tensor_tensor(ra[:, 0], ra[:, 0], rev[:], ALU.mult).then_inc(route, 1)
                if z:
                    scaled(2)
                    dve.tensor_tensor(v[:, 1:2], v[:, 1:2], v[:, 1:2], ALU.mult).then_inc(scale, 1)
                if r:
                    routed(3)
                    dve.tensor_reduce(m12[:, 1], ra[:, 0], AX.X, ALU.max).then_inc(route, 1)
                if z:
                    scaled(3)
                    dve.tensor_scalar(v[:], v[:], 1e-30, None, ALU.max).then_inc(scale, 1)
                if r:
                    routed(4)
                    dve.tensor_tensor(ra[:, 1], rev[:], bc(m12[:, 1]), ALU.is_equal).then_inc(route, 1)
                if z:
                    scaled(4)
                    dve.tensor_scalar(pw[:].bitcast(I32), v[:].bitcast(I32), 0x7F800000, None, ALU.bitwise_and).then_inc(scale, 1)
                if r:
                    routed(5)
                    dve.scalar_tensor_tensor(ra[:, 2], ra[:, 1], -3e38, L, ALU.mult, ALU.add).then_inc(route, 1)
                if z:
                    scaled(5)
                    dve.reciprocal(rp[:], pw[:]).then_inc(scale, 1)
                if r:
                    routed(6)
                    dve.tensor_reduce(m12[:, 2], ra[:, 2], AX.X, ALU.max).then_inc(route, 1)
                if z:
                    scaled(6)
                    dve.tensor_scalar(kk[:, S1:S1 + 1], rp[:, 0:1], TOP, None, ALU.mult).then_inc(scale, 1)
                    dve.tensor_scalar(kk[:, S2:S2 + 1], rp[:, 2:3], TOP, None, ALU.mult)
                if r:
                    routed(7)
                    dve.tensor_tensor(ra[:, 0], ra[:, 2], bc(m12[:, 2]), ALU.is_equal).then_inc(route, 1)
                if z:
                    dve.tensor_scalar(kk[:, I1:I1 + 1], pw[:, 0:1], 1.0 / TOP, None, ALU.mult)
                    dve.tensor_tensor(kk[:, C2:C2 + 1], pw[:, 0:1], rp[:, 1:2], ALU.mult)
                if r:
                    routed(8)
                    dve.tensor_tensor(ra[:, 0], ra[:, 0], rev[:], ALU.mult).then_inc(route, 1)
                if z:
                    dve.scalar_tensor_tensor(kk[:, CY:CY + 1], pw[:, 1:2], TOP ** -2, pw[:, 2:3], ALU.mult, ALU.mult)
                    scaled(7)
                    dve.tensor_scalar(beta[:, bass.ds(e, 1)].rearrange("p a f -> p (a f)"),
                                      b1t[:, bass.ds(e, 1), HK:].rearrange("p a f -> p (a f)"), kk[:, S1:S1 + 1], None,
                                      ALU.mult).then_inc(scale, 1)
                if r:
                    routed(9)
                    dve.tensor_reduce(m12[:, 3], ra[:, 0], AX.X, ALU.max).then_inc(route, 1)
                    routed(10)
                    dve.tensor_tensor(ra[:, 3], rev[:], bc(m12[:, 3]), ALU.is_equal).then_inc(route, 1)
                    dve.tensor_tensor(m12[:, 4], m12[:, 0], m12[:, 2], ALU.subtract)
                    routed(11)
                    dve.tensor_tensor(M[:, q], ra[:, 1], ra[:, 3], ALU.add).then_inc(route, 1)
                    dve.tensor_tensor(ra[:, 4], ra[:, 1], ra[:, 3], ALU.subtract).then_inc(route, 1)
                    routed(13)
                    dve.tensor_tensor(xrow[:, q * GROUP:(q + 1) * GROUP, :, 2 * D:].bitcast(F32).rearrange("p b j e -> p (b j) e"),
                                      ra[:, 4], bc(m12[:, 4]), ALU.mult).then_inc(route, 1)

            def route_2(g, q):
                dve.wait_ge(rank_ready, g + 1)
                dve.tensor_reduce(Mg[:], M[:, q].rearrange("p t e -> p e t"), AX.X, ALU.add).then_inc(route, 1)
                dve.tensor_tensor(ra[:, 5], rkp, ebase[:], ALU.add).then_inc(route, 1)
                dve.wait_ge(route, g * NROUTE + 16)
                dve.tensor_tensor(Macc[:, 1 - q], Macc[:, q], Mg[:], ALU.add)
                dve.tensor_copy(gids[:, q], ids[:, bass.ds(g * TILES, TILES)])
                dve.tensor_tensor(ra[:, 1], ra[:, 1], ra[:, 5], ALU.mult)
                dve.tensor_tensor(ra[:, 3], ra[:, 3], ra[:, 5], ALU.mult).then_inc(route, 1)
                dve.wait_ge(route, g * NROUTE + 17)
                if True:
                    with nc.allow_low_precision("places are integers below 2**17, exact in float32"):
                        dve.tensor_reduce(slots[:, q, 0], ra[:, 1], AX.X, ALU.add)
                        dve.tensor_reduce(slots[:, q, 1], ra[:, 3], AX.X, ALU.add).then_inc(route, 1)

            def step(i, s, g):
                p, o = s % 2, 1 - s % 2
                if live(s, 1) or live(s, 3):
                    a, z = (0 if live(s, 1) else J), (2 * J if live(s, 3) else J)
                    dve.wait_ge(sd_ready, i)
                    dve.reciprocal(rs[:, o, a:z], sd[:, o, a:z]).then_inc(rs_ready, 1)
                    dve.wait_ge(rs_ready, i)
                    dve.scalar_tensor_tensor(nmr[:, o, a:z], mv[:, o, a:z, 0], -1.0, rs[:, o, a:z], ALU.mult, ALU.mult).then_inc(nmr_ready, 1)
                if live(s, 0):
                    dve.wait_ge(x_in[s % 4], (i - s % 4) * 4 + 16)
                    for j in range(J):
                        dve.bn_stats(st[:, p, j], xin[:, s % 4, j]).then_inc(bn1, 1)
                if live(s, 2):
                    dve.wait_ge(g_ready, i - 1)
                    if s >= 6:
                        dve.wait_ge(x2_stored[(s - 2) % 4], (i - 2 - (s - 2) % 4) * 4)
                    dve.tensor_tensor(x2[:, (s - 2) % 4], g_bank(s % 2), xin[:, (s - 2) % 4], ALU.add).then_inc(x2_ready, 1)
                if live(s, 0):
                    hold(dve, bn1, (i + 1) * J)
                    for j in range(J):
                        dve.bn_aggr(mv[:, p, j], st[:, p, j]).then_inc(mv1, 1)
                if live(s, 2):
                    dve.wait_ge(x2_ready, i - 1)
                    for j in range(J):
                        dve.bn_stats(st[:, p, J + j], x2[:, (s - 2) % 4, j]).then_inc(bn2, 1)
                if live(s, 3):
                    dve.wait_ge(hi_ready, i - 2)
                    dve.wait_ge(xn2_ready, (i - 2) * J)
                    if s - 3 >= 2 * GROUP and (s - 3) % GROUP == 0:
                        dve.wait_ge(row_stored[((s - 3) // GROUP) % 2], bufcount(i - 3, s - 3))
                    r = xrow[:, (s - 3) % 8]
                    dve.tensor_tensor(r[:, :, D:2 * D], xn2[:, o], r[:, :, 0:D], ALU.subtract).then_inc(lo_ready, 1)
                if live(s, 2):
                    hold(dve, bn2, (i - 1) * J)
                    for j in range(J):
                        dve.bn_aggr(mv[:, p, J + j], st[:, p, J + j]).then_inc(mv2, 1)
                if s % GROUP >= 2 and live(s - s % GROUP, 4):
                    q, u, e = (s // GROUP - 1) % 2, s % GROUP - 2, g - 1
                    for k, (dst, c, a, n) in enumerate(((w1_half, S1, 0, W1N // 2), (w2_half, S2, W1N, W2N // 2))):
                        dve.wait_ge(whi_ready, e * 4 + 2 * u + k + 1)
                        dve.scalar_tensor_tensor(dst(e, 1, u), stage[:, q, a + u * n:a + (u + 1) * n], kcol(e, c),
                                                 dst(e, 0, u), ALU.mult, ALU.subtract).then_inc(wlo_ready, 1)
                if live(s, 5):
                    c = (s - 5) % GROUP * J
                    dve.wait_ge(lgp_ready, i - 4)
                    dve.tensor_tensor(lg[:, ((s - 5) // GROUP) % 2, c:c + J], lgp,
                                      rb[:].rearrange("p (a e) -> p a e", a=1).broadcast_to([P, J, E]), ALU.add).then_inc(lg_ready, 1)
                if s % GROUP == 0:
                    if live(s, 8):
                        dve.wait_ge(lg_ready, (g - 1) * GROUP)
                    if live(s, 8) or live(s, 4):
                        route_and_scales(g - 2 if live(s, 8) else None, (s // GROUP) % 2,
                                         g - 1 if live(s, 4) else None, (s // GROUP - 1) % 2)
                if s % GROUP == 1 and live(s, 9):
                    dve.wait_ge(scattered[(s // GROUP) % 2], parcount(g, s))
                    route_2(g - 2, (s // GROUP) % 2)
                if live(s, 0) and s % GROUP >= 2:
                    q, u = (s // GROUP) % 2, s % GROUP - 2
                    dve.wait_ge(w_in[q], (g - q) * 32 + 32 * (u + 1))
                    if u == 0:
                        if s >= 8:
                            dve.wait_ge(ar_ready, g - 1)
                        dve.tensor_reduce(am[:, q, 4:5], b1t[:, bass.ds(g, 1)].rearrange("p a f -> p (a f)"), AX.X, ALU.max,
                                          apply_absolute_value=True).then_inc(am_ready, 1)
                    dve.tensor_reduce(am[:, q, u:u + 1], stage[:, q, u * 1024:(u + 1) * 1024], AX.X, ALU.max,
                                      apply_absolute_value=True).then_inc(am_ready, 1)

            def parcount(g, s):
                q = (s // GROUP) % 2
                return (g - 2 - q) * (16 * 2 * TILES // 2) + 16

            phase_a(dve, step)

            n = [0]

            def go(ins):
                ins.then_inc(blk, 1)
                n[0] += 1
                dve.wait_ge(blk, n[0])

            def be(ap, m):
                return ap.rearrange("p (a e) -> p a e", a=1).broadcast_to([1, m, E])
            dve.wait_ge(tot_ready, 1)
            go(dve.tensor_copy(nb[:, 0], totp[0:1, :]))
            go(dve.tensor_tensor(cmp1, nb[:, 0].rearrange("p (e a) -> p e a", a=1).broadcast_to([1, E, 32]),
                                 steps_f[:, 0:32].rearrange("p (a s) -> p a s", a=1).broadcast_to([1, E, 32]), ALU.is_gt))
            go(dve.tensor_reduce(nb[:, 1], cmp1, AX.X, ALU.add))
            go(dve.tensor_tensor_scan(nb[:, 2], ones8[:], nb[:, 1], 0.0, ALU.mult, ALU.add))
            go(dve.tensor_tensor(cmp2[:, 0], steps_f[:, 32:].rearrange("p (b a) -> p b a", a=1).broadcast_to([1, MAX_BLOCKS, E]),
                                 be(nb[:, 2], MAX_BLOCKS), ALU.is_ge))
            go(dve.tensor_reduce(bl[:, 0], cmp2[:, 0], AX.X, ALU.add))
            go(dve.tensor_tensor(cmp2[:, 1], cmp2[:, 0], be(nb[:, 1], MAX_BLOCKS), ALU.mult))
            go(dve.tensor_reduce(bl[:, 1], cmp2[:, 1], AX.X, ALU.add))
            go(dve.tensor_tensor(bl[:, 2], steps_f[:, 32:], bl[:, 1], ALU.subtract))
            go(dve.scalar_tensor_tensor(info[:, 1, 0:MAX_BLOCKS], bl[:, 0], float(TOKENS // BLOCK), bl[:, 2], ALU.mult, ALU.add))
            dve.memset(info[:, 1, MAX_BLOCKS:], 0)
            dve.memset(info[:, 0, MAX_BLOCKS:], 0).then_inc(blk, 1)
            go(dve.tensor_scalar(info[:, 0, 0:MAX_BLOCKS], bl[:, 0], float(E - 1), None, ALU.min))

            def xt(b, k):
                dve.wait_ge(XTp_ready, b + 1)
                if k >= 2:
                    dve.wait_ge(h_ready, (b - 1) * HK)
                dve.tensor_copy(XT[:, k % 2], xTp).then_inc(XT_ready, 1)

            def front(b, k):
                e = dve.value_load(info[0:1, 0, bass.ds(b, 1)], min_val=0, max_val=E - 1)
                for f in range(HK):
                    dve.wait_ge(act_ready, b * HK + f + 1)
                    if k >= 2 and f == 0:
                        dve.wait_ge(ahi_ready, b - 1)
                        dve.wait_ge(alo_ready, b - 1)
                    dve.scalar_tensor_tensor(prod[:, k % 2, f], bank[f][:, BLOCK:], beta[:, bass.ds(e, 1), f:f + 1].rearrange("p a f -> p (a f)"),
                                             act1[:, f], ALU.add, ALU.mult).then_inc(prod_ready, 1)
                    if f == 1:
                        if isinstance(b, int) and b + 1 >= MAX_BLOCKS:
                            continue
                        xt(b + 1, k + 1)
                dve.wait_ge(ahi_ready, b + 1)
                dve.scalar_tensor_tensor(ab[:, k % 2, 1], prod[:, k % 2], kcol(e, C2), ab[:, k % 2, 0], ALU.mult, ALU.subtract).then_inc(alo_ready, 1)

            def back(b, k):
                e = dve.value_load(info[0:1, 0, bass.ds(b, 1)], min_val=0, max_val=E - 1)
                dve.wait_ge(y_ready, b + 1)
                if k >= 2:
                    dve.wait_ge(y2_ready, (b - 1) * J)
                dve.scalar_tensor_tensor(y1[:, k % 2], bank[5 + k % 2][:].rearrange("p (j d) -> p j d", j=J), kcol(e, CY),
                                         b2t[:, bass.ds(e, 1)].broadcast_to([P, J, D]), ALU.mult, ALU.add).then_inc(y1_ready, 1)
            xt(0, 0)
            phase_b(dve, front, back)

        @block.tensor
        def _(pe):
            def step(i, s, g):
                if s == 0:
                    pe.wait_ge(const_pool, 12)
                    pe.wait_ge(small_in, 16 * 8)
                    for m in range(J):
                        mm = pe.matmul(bank[7][:, 0:NODES], ones_f[:], At[:, m], start=(m == 0), stop=(m == J - 1))
                    mm.then_inc(degree_ready, 1)
                    pe.wait_ge(const_dve, CONST_DVE)
                if live(s, 2):
                    pe.wait_ge(ts_ready, i - 1)
                    if s >= 4:
                        pe.wait_ge(x2_ready, i - 3)
                    for j in range(J):
                        for k in range(DK):
                            mm = pe.matmul(g_bank(s % 2)[:, j], ts[:, s % 2, k, j * P:(j + 1) * P], Wg[:, k], start=(k == 0), stop=False)
                        mm = pe.matmul(g_bank(s % 2)[:, j], ones_b[:], bias_rows[:], start=False, stop=True)
                    mm.then_inc(g_ready, 1)
                if live(s, 5):
                    pe.wait_ge(xT_ready, i - 4)
                    if s >= 6:
                        pe.wait_ge(lg_ready, i - 5)
                    for j in range(J):
                        n = 0
                        for lx, lw in ((0, 0), (0, 1), (1, 0)):
                            for k in range(DK):
                                mm = pe.matmul(lgp[:, j], xT[:, (s - 5) % 2 ^ 0, lx, k, j * P:(j + 1) * P], rw16[:, lw, k], start=(n == 0), stop=(n == 5))
                                n += 1
                    mm.then_inc(lgp_ready, 1)
                if live(s, 4):
                    pe.wait_ge(lo_ready, i - 3)
                    pe.wait_ge(hi_ready, i - 3)
                    if s >= 5:
                        pe.wait_ge(xT_ready, i - 4)
                    for l in range(2):
                        for k in range(DK):
                            for j in range(J):
                                mm = pe.transpose(xTp[:, l, k, j * P:(j + 1) * P], xrow[:, (s - 4) % 8, j, l * D + k * P:l * D + (k + 1) * P], ident[:])
                    mm.then_inc(xTp_ready, 1)
                if s % GROUP == 1 and live(s, 9):
                    q = (s // GROUP) % 2
                    pe.wait_ge(route, (g - 2) * NROUTE + 12)
                    pe.matmul(rkp, tri[:], M[:, q], start=True, stop=False)
                    pe.matmul(rkp, ones[:], Macc[:, q].rearrange("p (a e) -> p a e", a=1).broadcast_to([P, TILES, E]), start=False, stop=False)
                    for c in range(TILES - 1):
                        mm = pe.matmul(rkp[:, c + 1:], ones[:], M[:, q, c:c + 1].broadcast_to([P, TILES - 1 - c, E]),
                                       start=False, stop=(c == TILES - 2))
                    mm.then_inc(rank_ready, 1)
                if live(s, 1):
                    pe.wait_ge(xn1_ready, i * J)
                    if s >= 3:
                        pe.wait_ge(ts_ready, i - 2)
                    for t in range(DK):
                        for m in range(J):
                            mm = pe.matmul(bank[(s - 1) % 2][:, t * NODES:(t + 1) * NODES], xn1[:, (s - 1) % 2, m, t * P:(t + 1) * P],
                                           At[:, m], start=(m == 0), stop=(m == J - 1))
                    mm.then_inc(t_ready, 1)
            phase_a(pe, step)
            pe.wait_ge(route, GROUPS * NROUTE)
            pe.matmul(totp, ones[:], Macc[:, GROUPS % 2], start=True, stop=True).then_inc(tot_ready, 1)

            pe.wait_ge(blk, 12)
            pe.wait_ge(wlo_ready, E * 4)
            pe.wait_ge(whi_ready, E * 4)

            def rows_t(b, k):
                pe.wait_ge(g_in[k % 4], (b - k % 4) * 8 + 32)
                if k >= 1:
                    pe.wait_ge(XT_ready, b)
                for l in range(2):
                    for c in range(DK):
                        for j in range(J):
                            mm = pe.transpose(xTp[:, l, c, j * P:(j + 1) * P], G[:, k % 4, j, l * D + c * P:l * D + (c + 1) * P], ident[:])
                mm.then_inc(XTp_ready, 1)

            def front(b, k):
                e = pe.value_load(info[0:1, 0, bass.ds(b, 1)], min_val=0, max_val=E - 1)
                pe.wait_ge(XT_ready, b + 1)
                for f in range(HK):
                    if k >= 1:
                        pe.wait_ge(prod_ready, (b - 1) * HK + f + 1)
                    for half in range(2):
                        n = 0
                        for c in range(DK):
                            for lw in range(2):
                                w = W1[:, bass.ds(e, 1), lw, c, half * H + f * P:half * H + (f + 1) * P].rearrange("p a n -> p (a n)")
                                for lx in range(2 - lw):
                                    mm = pe.matmul(bank[f][:, half * BLOCK:(half + 1) * BLOCK], w, XT[:, k % 2, lx, c], start=(n == 0), stop=(n == 5))
                                    n += 1
                    mm.then_inc(h_ready, 1)
                    if f == 1 and not (isinstance(b, int) and b + 1 >= MAX_BLOCKS):
                        rows_t(b + 1, k + 1)

            def back(b, k):
                e = pe.value_load(info[0:1, 0, bass.ds(b, 1)], min_val=0, max_val=E - 1)
                pe.wait_ge(ahi_ready, b + 1)
                pe.wait_ge(alo_ready, b + 1)
                if k >= 2:
                    pe.wait_ge(y1_ready, b - 1)
                n = 0
                for j in range(J):
                    n = 0
                    for c in range(HK):
                        for lw in range(2):
                            w = W2[:, bass.ds(e, 1), lw, c].rearrange("p a n -> p (a n)")
                            for la in range(2 - lw):
                                mm = pe.matmul(bank[5 + k % 2][:, j * D:(j + 1) * D], ab[:, k % 2, la, c, j * P:(j + 1) * P], w,
                                               start=(n == 0), stop=(n == 3 * HK - 1))
                                n += 1
                mm.then_inc(y_ready, 1)
            rows_t(0, 0)
            phase_b(pe, front, back)


def kernel(x, adj, L0_gnn_weight, L0_gnn_bias, L0_ffn_router_w, L0_ffn_router_b, L0_ffn_fc1_w, L0_ffn_fc1_b,
           L0_ffn_fc2_w, L0_ffn_fc2_b):
    import numpy as np
    import concourse.bacc as bacc
    from concourse.bass_utils import run_bass_kernel_spmd

    def tiles(a):
        a = np.asarray(a)
        return np.ascontiguousarray(a.reshape(a.shape[0] // P, P, a.shape[1]).transpose(1, 0, 2))

    fc1 = np.asarray(L0_ffn_fc1_w)
    fc2 = np.asarray(L0_ffn_fc2_w)
    arrays = {
        "x": np.ascontiguousarray(np.asarray(x).reshape(TOKENS, D)),
        "adj": tiles(adj),
        "adj_t": tiles(np.asarray(adj).T),
        "gnn_w": tiles(L0_gnn_weight),
        "gnn_b": np.asarray(L0_gnn_bias),
        "router_w": tiles(np.asarray(L0_ffn_router_w).T),
        "router_b": np.asarray(L0_ffn_router_b),
        "w1": np.ascontiguousarray(fc1.reshape(E, 2 * H, DK, P).transpose(0, 3, 2, 1).reshape(E, P, W1N)),
        "b1": np.ascontiguousarray(np.asarray(L0_ffn_fc1_b).reshape(E, FT, P).transpose(2, 0, 1)),
        "w2": np.ascontiguousarray(fc2.reshape(E, D, HK, P).transpose(0, 3, 2, 1).reshape(E, P, W2N)),
        "b2": np.asarray(L0_ffn_fc2_b),
    }
    nc = bacc.Bacc("TRN2", target_bir_lowering=False, num_devices=1)
    feed, args = {}, []
    for name, a in arrays.items():
        feed[f"in_{name}"] = a
        args.append(nc.dram_tensor(f"in_{name}", a.shape, mybir.dt.from_np(a.dtype), kind="ExternalInput").ap())
    out = nc.dram_tensor("out", (TOKENS + BLOCK, D), F32, kind="ExternalOutput").ap()
    program(nc, *args, out)
    r = run_bass_kernel_spmd(nc, [feed], core_ids=[0])
    return r.results[0]["out"][:TOKENS].reshape(BATCHES, NODES, D)
```

```python
from contextlib import ExitStack

import concourse.bass as bass
from concourse import mybir

F32 = mybir.dt.float32
F16 = mybir.dt.float16
BF16 = mybir.dt.bfloat16
I32 = mybir.dt.int32
ALU = mybir.AluOpType
ACT = mybir.ActivationFunctionType
AX = mybir.AxisListType

P = 128
D = 256
DK = D // P
BATCHES = 32
NODES = 256
J = NODES // P
TOKENS = BATCHES * NODES
E = 8
H = 512
HK = H // P
FT = 2 * H // P
BLOCK = 256
MAX_BLOCKS = (2 * TOKENS + E * (BLOCK - 1)) // BLOCK
GROUP = 4
TILES = GROUP * J
GROUPS = BATCHES // GROUP
EARLY = GROUPS - 2
EARLY_BLOCKS = -((E * (BLOCK - 1) - 2 * EARLY * GROUP * NODES) // BLOCK)
LATE_BLOCKS = MAX_BLOCKS - EARLY_BLOCKS
TABLE = E * TOKENS + MAX_BLOCKS * BLOCK
ROW = D + E
W1N = DK * 2 * H
W2N = HK * D
EPS = 1e-5
TOP = 2.0 ** 14
S1, I1, C2, S2, CY = range(5)

IDX_RING = 8
AHEAD = 4
CONST_DVE = 9
NCHAIN = 8
NROUTE = 18


def program(nc, x, adj, adj_t, gnn_w, gnn_b, router_w, router_b, w1, b1, w2, b2, out):
    x_v = x.rearrange("(b j p) d -> b p j d", j=J, p=P)
    out_v = out.rearrange("(b j p) d -> b p j d", j=J, p=P)
    rows = nc.dram_tensor("rows", (TOKENS + BLOCK, ROW), I32, kind="Internal").ap()
    rows_v = rows.rearrange("(g t p) c -> g p t c", t=2, p=P)
    table = nc.dram_tensor("table", (TABLE, 1), I32, kind="Internal").ap()
    table_b = table.rearrange("(b p j) o -> b p (j o)", p=P, j=2)

    with ExitStack() as ctx:
        def sb(name, shape, dt=F32):
            return ctx.enter_context(nc.sbuf_tensor(name, shape, dt))

        def sem(name):
            return ctx.enter_context(nc.semaphore(name))

        bank = [ctx.enter_context(nc.psum_tensor(f"bank{i}", [P, 512], F32)) for i in range(8)]

        W1 = sb("W1", [P, E, 2, DK, 2 * H], F16)
        W2 = sb("W2", [P, E, 2, HK, D], F16)
        stage = sb("stage", [P, 2, W1N + W2N])
        ident = sb("ident", [P, P], F16)
        ident_f = sb("ident_f", [P, P])
        tri = sb("tri", [P, P], F16)
        ones = sb("ones", [P, P], F16)
        ones_b = sb("ones_b", [P, P], BF16)
        ones_f = sb("ones_f", [P, P])
        eps = sb("eps", [P, 1])
        ids = sb("ids", [P, BATCHES * J], I32)
        iota_i = sb("iota_i", [P, 2, TILES, E], I32)
        rev = sb("rev", [P, TILES, E])
        ebase = sb("ebase", [P, TILES, E])
        steps_i = sb("steps_i", [1, 32 + MAX_BLOCKS], I32)
        steps_f = sb("steps_f", [1, 32 + MAX_BLOCKS])
        pad_out = sb("pad_out", [P, TABLE // P], I32)
        zeros = sb("zeros", [P, 2, ROW], I32)
        ones8 = sb("ones8", [1, E])
        adj_n = sb("adj_n", [P, J, NODES])
        At = sb("At", [P, J, NODES])
        Wg = sb("Wg", [P, DK, D])
        bg = sb("bg", [P, D])
        rw = sb("rw", [P, DK, E])
        rb = sb("rb", [P, E])
        b1t = sb("b1t", [P, E, FT])
        b2t = sb("b2t", [P, E, D])
        deg = sb("deg", [P, 2, J + NODES])
        bias_rest = sb("bias_rest", [P, D])
        bias_part = sb("bias_part", [P, 3, D], BF16)
        bias_rows = sb("bias_rows", [P, D], BF16)
        xin = sb("xin", [P, 4, J, D])
        st = sb("st", [P, 2, 2 * J, 6])
        mv = sb("mv", [P, 2, 2 * J, 2])
        sd = sb("sd", [P, 2, 2 * J])
        rs = sb("rs", [P, 2, 2 * J])
        nmr = sb("nmr", [P, 2, 2 * J])
        xn1 = sb("xn1", [P, 2, J, D])
        ts = sb("ts", [P, 2, DK, NODES])
        x2 = sb("x2", [P, 4, J, D])
        xrow = sb("xrow", [P, 2 * GROUP, J, ROW])
        xT = sb("xT", [P, 2, DK, NODES])
        pad_ids = xT[:].rearrange("p a k n -> p (a k n)").bitcast(I32)[:, 0:TABLE // P]
        lg = sb("lg", [P, 2, TILES, E])
        m12 = sb("m12", [P, 5, TILES])
        ra = sb("ra", [P, 6, TILES, E])
        M = sb("M", [P, 2, TILES, E], F16)
        Mg = sb("Mg", [P, E])
        Macc = sb("Macc", [P, 2, E], F16)
        gids = sb("gids", [P, 2, TILES], I32)
        slots = sb("slots", [P, 2, 2, TILES], I32)
        am = sb("am", [P, 2, 5])
        ar = sb("ar", [P, 2, 5])
        junk = sb("junk", [P, W2N // 2], BF16)
        v = sb("v", [P, 3])
        pw = sb("pw", [P, 3])
        rp = sb("rp", [P, 3])
        K = sb("K", [P, E, 5])
        beta = sb("beta", [P, E, HK])
        nb = sb("nb", [1, 9, E])
        spare = xin[0:1].rearrange("p a j d -> p (a j d)")
        cmp1 = spare[:, 0:32 * E].rearrange("p (e s) -> p e s", e=E)
        cmp2 = spare[:, 32 * E:(32 + MAX_BLOCKS) * E].rearrange("p (b e) -> p b e", e=E)
        bl = sb("bl", [1, 3, MAX_BLOCKS])
        early = sb("early", [1, 2, MAX_BLOCKS])
        late = sb("late", [1, 3, 2, LATE_BLOCKS])
        info = sb("info", [1, 2, MAX_BLOCKS + 1], I32)
        idx = sb("idx", [P, IDX_RING, 2], I32)
        G = xrow[:, 0:4]
        parts = sb("parts", [P, 2, J, 2 * D], F16)
        XT = xn1[:].rearrange("p a j d -> p (a j d)").bitcast(F16).rearrange("p (a l k n) -> p a l k n", a=2, l=2, k=DK)
        free = stage[:].rearrange("p a n -> p (a n)")
        N = HK * BLOCK
        act1 = free[:, 0:N].rearrange("p (f n) -> p f n", f=HK)
        prod = free[:, N:3 * N].rearrange("p (a f n) -> p a f n", a=2, f=HK)
        ab = free[:, 3 * N:5 * N].bitcast(F16).rearrange("p (a l f n) -> p a l f n", a=2, l=2, f=HK)
        th = sb("th", [P, 2, 2])
        cw = sb("cw", [P, 2, 2])
        y1 = xin[:, 2:4]
        y2 = x2[:, 0:2]

        def g_bank(b2):
            return bank[2 + b2][:].rearrange("p (j d) -> p j d", j=J)

        xnTp = bank[4][:].rearrange("p (k n) -> p k n", k=DK)
        xTp = bank[4][:].bitcast(F16).rearrange("p (l k n) -> p l k n", l=2, k=DK)
        lgp = bank[5][:, 0:J * E].rearrange("p (j e) -> p j e", j=J)
        rkp = bank[6][:, 0:TILES * E].rearrange("p (t e) -> p t e", t=TILES)
        totp = bank[7][:, 0:2 * E].rearrange("p (a e) -> p a e", a=2)

        adj_in = sem("adj_in")
        small_in = sem("small_in")
        expert_in = sem("expert_in")
        x_in = [sem(f"x_in{i}") for i in range(4)]
        w_in = [sem(f"w_in{i}") for i in range(2)]
        const_pool = sem("const_pool")
        const_dve = sem("const_dve")
        pad_out_ready = sem("pad_out_ready")
        deg_root = sem("deg_root")
        pad_stored = sem("pad_stored")
        degree_ready = sem("degree_ready")
        bn1 = sem("bn1")
        bn2 = sem("bn2")
        mv1 = sem("mv1")
        mv2 = sem("mv2")
        sd_ready = sem("sd_ready")
        rs_ready = sem("rs_ready")
        nmr_ready = sem("nmr_ready")
        xn1_ready = sem("xn1_ready")
        t_ready = sem("t_ready")
        ts_ready = sem("ts_ready")
        g_ready = sem("g_ready")
        x2_ready = sem("x2_ready")
        x2_stored = [sem(f"x2_stored{i}") for i in range(4)]
        xn2_ready = sem("xn2_ready")
        xTp_ready = sem("xTp_ready")
        xT_ready = sem("xT_ready")
        lgp_ready = sem("lgp_ready")
        lg_ready = sem("lg_ready")
        route = sem("route")
        rank_ready = sem("rank_ready")
        row_stored = [sem(f"row_stored{i}") for i in range(2)]
        scattered = [sem(f"scattered{i}") for i in range(2)]
        am_ready = sem("am_ready")
        sum_ready = sem("sum_ready")
        ar_ready = sem("ar_ready")
        scale = sem("scale")
        whi_ready = sem("whi_ready")
        wlo_ready = sem("wlo_ready")
        tot_ready = sem("tot_ready")
        blk = sem("blk")
        early_listed = sem("early_listed")
        listed = sem("listed")
        idx_in = [sem(f"idx_in{i}") for i in range(IDX_RING)]
        g_in = [sem(f"g_in{i}") for i in range(4)]
        hi_ready = sem("hi_ready")
        lo_ready = sem("lo_ready")
        XTp_ready = sem("XTp_ready")
        XT_ready = sem("XT_ready")
        h_ready = sem("h_ready")
        act_ready = sem("act_ready")
        prod_ready = sem("prod_ready")
        ahi_ready = sem("ahi_ready")
        alo_ready = sem("alo_ready")
        y_ready = sem("y_ready")
        y1_ready = sem("y1_ready")
        th_ready = sem("th_ready")
        cw_ready = sem("cw_ready")
        y2_ready = sem("y2_ready")
        added = sem("added")

        block = ctx.enter_context(nc.Block())

        LAST = BATCHES + GROUP + 1

        def phase_a(eng, step):
            for i in range(8):
                step(i, i, i // GROUP)
            with eng.Fori(8 // GROUP, GROUPS - 1, 2) as g0:
                for u in range(8):
                    step(g0 * GROUP + u, 8 + u, g0 + u // GROUP)
            for i in range(BATCHES, LAST):
                step(i, i, i // GROUP)

        def live(s, back, n=BATCHES):
            return back <= s < n + back

        def hold(eng, sem, value):
            if not isinstance(value, int):
                value = eng.to_reg(value)
                eng.wait_ge(sem, 1)
            eng.wait_ge(sem, value)

        def bufcount(b, s):
            if isinstance(b, int):
                return 16 * ((b // GROUP) // 2)
            return (b - (s % 8)) * 2

        def kcol(e, c):
            return K[:, bass.ds(e, 1), c:c + 1].rearrange("p a c -> p (a c)")

        def w1_half(e, part, u):
            return W1[:].rearrange("p e l k f -> p e l (k f)")[:, bass.ds(e, 1), part, u * W1N // 2:(u + 1) * W1N // 2].rearrange("p a n -> p (a n)")

        def w2_half(e, part, u):
            return W2[:].rearrange("p e l k f -> p e l (k f)")[:, bass.ds(e, 1), part, u * W2N // 2:(u + 1) * W2N // 2].rearrange("p a n -> p (a n)")

        def phase_b(eng, front, back, last_step=None):
            front(0, 0)
            if last_step:
                last_step(LAST, LAST, LAST // GROUP)
            n = 4
            for b in range(1, n):
                front(b, b)
                back(b - 1, b - 1)
            eng.wait_ge(listed, 1)
            with eng.Fori(n, (MAX_BLOCKS - n) // 4 * 4 + 1, 4) as b0:
                for k in range(4):
                    front(b0 + k, n + k)
                    back(b0 + k - 1, n + k - 1)
            for b in range(n + (MAX_BLOCKS - n) // 4 * 4, MAX_BLOCKS):
                front(b, b)
                back(b - 1, b - 1)
            back(MAX_BLOCKS - 1, MAX_BLOCKS - 1)

        @block.sync
        def _(sp):
            for dst, src in ((At, adj_t), (adj_n, adj)):
                sp.dma_start(dst[:], src).then_inc(adj_in, 16)
            sp.dma_start(xin[:, 0], x_v[0]).then_inc(x_in[0], 16)
            for dst, src in ((Wg, gnn_w), (rw, router_w), (bg, gnn_b.rearrange("(a d) -> a d", a=1).broadcast_to([P, D])),
                             (rb, router_b.rearrange("(a d) -> a d", a=1).broadcast_to([P, E]))):
                sp.dma_start(dst[:], src).then_inc(small_in, 16)

            def load_w(g, q, u):
                for src, a, n in ((w1, 0, W1N // 2), (w2, W1N, W2N // 2)):
                    sp.dma_start(stage[:, q, a + u * n:a + (u + 1) * n],
                                 src[bass.ds(g, 1), :, u * n:(u + 1) * n].rearrange("a p n -> p (a n)")).then_inc(w_in[q], 16)

            def load_idx(b, k):
                start = sp.value_load(info[0:1, 1, bass.ds(b, 1)], min_val=0, max_val=TABLE // BLOCK - 1)
                sp.dma_start(idx[:, k], table_b[bass.ds(start, 1)].rearrange("a p j -> p (a j)")).then_inc(idx_in[k], 16)

            def step(i, s, g):
                if s == 3:
                    sp.dma_start(b1t[:], b1).then_inc(expert_in, 16)
                    sp.dma_start(b2t[:], b2.rearrange("(a e) d -> a e d", a=1).broadcast_to([P, E, D])).then_inc(expert_in, 16)
                if live(s, 0) and s > 0:
                    if s >= 4:
                        hold(sp, x2_ready, i - 3)
                    sp.dma_start(xin[:, s % 4], x_v[bass.ds(i, 1)].rearrange("a p j d -> p (a j) d")).then_inc(x_in[s % 4], 16)
                if s % GROUP < 2 and live(s, 0):
                    u = s % GROUP
                    if s >= 2 * GROUP:
                        sp.wait_ge(whi_ready, (g - 2) * 4 + 2 * u + 2)
                        hold(sp, wlo_ready, (g - 2) * 4 + 2 * u + 2)
                    load_w(g, (s // GROUP) % 2, u)
                if live(s, 3):
                    hold(sp, x2_ready, i - 2)
                    sp.dma_start(out_v[bass.ds(i - 3, 1)].rearrange("a p j d -> p (a j) d"), x2[:, (s - 3) % 4]).then_inc(x2_stored[(s - 3) % 4], 16)
                if s % GROUP == 2 and live(s, 10, BATCHES - GROUP) or s == LAST:
                    hold(sp, route, (g - 2) * NROUTE + 14)
                    hold(sp, xn2_ready, (g - 1) * GROUP * J)
                    q = (s // GROUP) % 2
                    sp.dma_start(rows_v[bass.ds((g - 2) * GROUP, GROUP)].rearrange("b p j c -> p b j c"),
                                 xrow[:, q * GROUP:(q + 1) * GROUP].bitcast(I32)).then_inc(row_stored[q], 16)
                if s == BATCHES + 2:
                    sp.wait_ge(early_listed, 1)
                    for q in range(2):
                        sp.wait_ge(scattered[q], 16 + 16 * 2 * TILES * ((EARLY + 1 - q) // 2))
                    for b in range(IDX_RING):
                        load_idx(b, b)
            sp.wait_ge(const_pool, 1)
            sp.dma_start(rows_v[BATCHES], zeros[:]).then_inc(pad_stored, 16)
            sp.dma_start(out_v[BATCHES], zeros[:, :, 0:D].bitcast(F32)).then_inc(pad_stored, 16)
            phase_a(sp, step)
            step(LAST, LAST, LAST // GROUP)

            early_end = EARLY_BLOCKS // IDX_RING * IDX_RING
            full = MAX_BLOCKS // IDX_RING * IDX_RING

            def load_more(first, end):
                with sp.Fori(first, end, IDX_RING) as b0:
                    for k in range(IDX_RING):
                        hold(sp, added, (b0 + k - IDX_RING + 1) * 32)
                        load_idx(b0 + k, k)
            load_more(IDX_RING, early_end)
            sp.wait_ge(listed, 1)
            for q in scattered:
                sp.wait_ge(q, 16 + 16 * 2 * TILES * GROUPS // 2)
            load_more(early_end, full)
            for b in range(full, MAX_BLOCKS):
                sp.wait_ge(added, (b - IDX_RING + 1) * 32)
                load_idx(b, b % IDX_RING)
            sp.wait_ge(added, MAX_BLOCKS * 32)

        @block.gpsimd
        def _(pool):
            pool.memset(zeros[:], 0).then_inc(const_pool, 1)
            pool.memset(ones[:], 1.0).then_inc(const_pool, 1)
            pool.memset(ones_f[:], 1.0).then_inc(const_pool, 1)
            pool.memset(ones_b[:], 1.0).then_inc(const_pool, 1)
            pool.iota(pad_ids, pattern=[[1, TABLE // P]], base=0, channel_multiplier=TABLE // P).then_inc(const_pool, 1)
            pool.iota(ids[:], pattern=[[P, BATCHES * J]], base=0, channel_multiplier=1).then_inc(const_pool, 1)
            pool.iota(iota_i[:, 0], pattern=[[0, TILES], [-1, E]], base=E, channel_multiplier=0).then_inc(const_pool, 1)
            pool.iota(iota_i[:, 1], pattern=[[0, TILES], [TOKENS, E]], base=0, channel_multiplier=0).then_inc(const_pool, 1)
            pool.iota(steps_i[:, 0:32], pattern=[[BLOCK, 32]], base=0, channel_multiplier=0).then_inc(const_pool, 1)
            pool.iota(steps_i[:, 32:], pattern=[[1, MAX_BLOCKS]], base=0, channel_multiplier=0).then_inc(const_pool, 1)
            pool.wait_ge(const_pool, 10)
            pool.affine_select(out=tri[:], in_=ones[:], pattern=[[1, P]], compare_op=ALU.is_gt, fill=0.0,
                               base=0, channel_multiplier=-1).then_inc(const_pool, 1)
            pool.affine_select(out=ident[:], in_=ones[:], pattern=[[1, P]], compare_op=ALU.is_equal, fill=0.0,
                               base=0, channel_multiplier=-1).then_inc(const_pool, 1)
            pool.affine_select(out=ident_f[:], in_=ones_f[:], pattern=[[1, P]], compare_op=ALU.is_equal, fill=0.0,
                               base=0, channel_multiplier=-1).then_inc(const_pool, 1)
            pool.wait_ge(pad_out_ready, 1)
            half = TABLE // P // 2
            for q in range(2):
                pool.dma_start(table.rearrange("(p c) o -> p (c o)", p=P)[:, q * half:(q + 1) * half],
                             pad_out[:, q * half:(q + 1) * half]).then_inc(scattered[q], 16)
            for q in scattered:
                pool.wait_ge(q, 16)

            def scatter(q, c):
                for k in range(2):
                    pool.indirect_dma_start(
                        table, bass.IndirectOffsetOnAxis(ap=slots[:, q, k, c:c + 1], axis=0),
                        gids[:, q, c:c + 1], None).then_inc(scattered[q], 16)

            def step(i, s, g):
                if s % GROUP == 3 and live(s, 0):
                    hold(pool, am_ready, (g + 1) * 3)
                    hold(pool, sum_ready, (g + 1) * 2)
                    q = (s // GROUP) % 2
                    pool.partition_all_reduce(ar[:, q], am[:, q], P, bass.bass_isa.ReduceOp.max).then_inc(ar_ready, 1)
                if s % GROUP in (2, 3) and live(s - s % GROUP, 8, EARLY * GROUP):
                    if s % GROUP == 2:
                        hold(pool, route, (g - 1) * NROUTE)
                    first = (s % GROUP - 2) * TILES // 2
                    for c in range(first, first + TILES // 2):
                        scatter((s // GROUP) % 2, c)
            phase_a(pool, step)

            pool.wait_ge(row_stored[0], 16 * GROUPS // 2)
            pool.wait_ge(row_stored[1], 16 * EARLY // 2)

            def gather(b, k):
                hold(pool, idx_in[k % IDX_RING], (b - k % IDX_RING) * 2 + 16)
                if k >= 4:
                    hold(pool, lo_ready, b - 3)
                    pool.wait_ge(th_ready, b - 3)
                for j in range(J):
                    pool.indirect_dma_start(G[:, k % 4, j].bitcast(I32), None, rows,
                                            bass.IndirectOffsetOnAxis(ap=idx[:, k % IDX_RING, j:j + 1], axis=0)).then_inc(g_in[k % 4], 16)

            def add(b, k):
                pool.wait_ge(y2_ready, (b + 1) * J)
                if k >= 1:
                    hold(pool, added, b * 32)
                for j in range(J):
                    pool.indirect_dma_start(out, bass.IndirectOffsetOnAxis(ap=idx[:, k % IDX_RING, j:j + 1], axis=0),
                                            y2[:, k % 2, j], None, compute_op=ALU.add).then_inc(added, 16)

            def scatter_late(n):
                g = EARLY + n // TILES
                if n % TILES == 0:
                    pool.wait_ge(route, (g + 1) * NROUTE)
                scatter(g % 2, n % TILES)

            for b in range(AHEAD):
                gather(b, b)
            for c in range(TILES // 2):
                scatter_late(c)
            first = AHEAD + 1 + TILES // 2
            for b in range(AHEAD, first):
                gather(b, b)
                if b == AHEAD:
                    for c in range(TILES // 2, TILES):
                        scatter_late(c)
                    pool.wait_ge(pad_stored, 16 * 2)
                    for s in x2_stored:
                        pool.wait_ge(s, 16 * BATCHES // 4)
                else:
                    for c in range(2):
                        scatter_late(TILES + 2 * (b - AHEAD - 1) + c)
                add(b - AHEAD, b - AHEAD)
            pool.wait_ge(row_stored[1], 16 * GROUPS // 2)
            full = (MAX_BLOCKS - first) // IDX_RING * IDX_RING + first
            with pool.Fori(first, full, IDX_RING) as b0:
                for k in range(IDX_RING):
                    gather(b0 + k, first + k)
                    add(b0 + k - AHEAD, first + k - AHEAD)
            for b in range(full, MAX_BLOCKS):
                gather(b, b)
                add(b - AHEAD, b - AHEAD)
            for b in range(MAX_BLOCKS - AHEAD, MAX_BLOCKS):
                add(b, b)

        @block.scalar
        def _(act):
            act.wait_ge(const_dve, 3)
            act.activation(deg[:, 0], deg[:, 0], ACT.Sqrt).then_inc(deg_root, 1)

            def step(i, s, g):
                p, o = s % 2, 1 - s % 2
                if live(s, 1):
                    act.wait_ge(nmr_ready, i)
                    if s >= 3:
                        act.wait_ge(t_ready, i - 2)
                    for j in range(J):
                        act.activation(xn1[:, o, j], xin[:, (s - 1) % 4, j], ACT.Identity, bias=nmr[:, o, j:j + 1],
                                       scale=rs[:, o, j:j + 1]).then_inc(xn1_ready, 1)
                if live(s, 3):
                    act.wait_ge(nmr_ready, i)
                    if s - 3 >= 2 * GROUP and (s - 3) % GROUP == 0:
                        act.wait_ge(row_stored[((s - 3) // GROUP) % 2], bufcount(i - 3, s - 3))
                    for j in range(J):
                        act.activation(xrow[:, (s - 3) % 8, j, 0:D], x2[:, (s - 3) % 4, j], ACT.Identity, bias=nmr[:, o, J + j:J + j + 1],
                                       scale=rs[:, o, J + j:J + j + 1]).then_inc(xn2_ready, 1)
                if live(s, 4):
                    act.wait_ge(xTp_ready, i - 3)
                    if s >= 6:
                        act.wait_ge(lgp_ready, i - 5)
                    act.activation(xT[:, s % 2], xnTp, ACT.Copy).then_inc(xT_ready, 1)
                if live(s, 0) or live(s, 2):
                    a, z = (0 if live(s, 0) else J), (2 * J if live(s, 2) else J)
                    if live(s, 0):
                        act.wait_ge(mv1, (i + 1) * J)
                    if live(s, 2):
                        act.wait_ge(mv2, (i - 1) * J)
                    if s == 0:
                        act.wait_ge(const_dve, 1)
                    if s >= 2:
                        act.wait_ge(rs_ready, i - 1)
                    act.activation(sd[:, p, a:z], mv[:, p, a:z, 1], ACT.Sqrt, bias=eps[:]).then_inc(sd_ready, 1)
                if live(s, 1):
                    act.wait_ge(t_ready, i)
                    if s >= 3:
                        act.wait_ge(g_ready, i - 2)
                    act.activation(ts[:, (s - 1) % 2], bank[(s - 1) % 2][:].rearrange("p (k n) -> p k n", k=DK), ACT.Copy).then_inc(ts_ready, 1)
                if s % GROUP in (1, 2) and live(s - s % GROUP, 4):
                    q, u, e = (s // GROUP - 1) % 2, s % GROUP - 1, g - 1
                    act.wait_ge(scale, g * NCHAIN)
                    for dst, c, a, n in ((w1_half, S1, 0, W1N // 2), (w2_half, S2, W1N, W2N // 2)):
                        act.activation(dst(e, 0, u), stage[:, q, a + u * n:a + (u + 1) * n], ACT.Copy, scale=kcol(e, c)).then_inc(whi_ready, 1)
                if live(s, 0) and s % GROUP >= 2:
                    q, u = (s // GROUP) % 2, s % GROUP - 2
                    act.wait_ge(w_in[q], (g - q) * 32 + 32 * (u + 1))
                    if u == 0 and s >= 8:
                        act.wait_ge(ar_ready, g - 1)
                    act.activation(junk[:], stage[:, q, W1N + u * 512:W1N + (u + 1) * 512], ACT.Abs,
                                   accum_out=am[:, q, 2 + u:3 + u]).then_inc(sum_ready, 1)
            phase_a(act, step)

            act.activation(junk[0:1, 0:1], eps[0:1], ACT.Silu)
            act.wait_ge(expert_in, 16 * 2)
            act.wait_ge(early_listed, 1)
            act.wait_ge(scale, E * NCHAIN)

            def expert(eng, b):
                return eng.value_load(info[0:1, 0, bass.ds(b, 1)], min_val=0, max_val=E - 1)

            def split_hi(b, k):
                act.wait_ge(g_in[k % 4], (b - k % 4) * 8 + 32)
                if k >= 2:
                    act.wait_ge(XTp_ready, b - 1)
                act.activation(parts[:, k % 2, :, 0:D], G[:, k % 4, :, 0:D], ACT.Copy).then_inc(hi_ready, 1)

            def front(b, k):
                e = expert(act, b)
                for f in range(HK):
                    act.wait_ge(h_ready, b * HK + f + 1)
                    if k >= 1:
                        act.wait_ge(prod_ready, (b - 1) * HK + f + 1)
                    act.activation(act1[:, f], bank[f][:, 0:BLOCK], ACT.Silu,
                                   bias=b1t[:, bass.ds(e, 1), f:f + 1].rearrange("p a f -> p (a f)"),
                                   scale=kcol(e, I1)).then_inc(act_ready, 1)
                    if f == 1 and not (isinstance(b, int) and b + 2 >= MAX_BLOCKS):
                        split_hi(b + 2, k + 2)
                if k >= 2:
                    act.wait_ge(cw_ready, b - 1)
                act.activation(th[:, k % 2], G[:, k % 4, :, D:][:, :, bass.ds(e, 1)].rearrange("p j a -> p (j a)"),
                               ACT.Tanh, scale=0.5).then_inc(th_ready, 1)
                act.wait_ge(prod_ready, (b + 1) * HK)
                if k >= 2:
                    act.wait_ge(y_ready, b - 1)
                act.activation(ab[:, k % 2, 0], prod[:, k % 2], ACT.Copy, scale=kcol(e, C2)).then_inc(ahi_ready, 1)
                act.wait_ge(th_ready, b + 1)
                if k >= 2:
                    act.wait_ge(y2_ready, (b - 1) * J)
                act.activation(cw[:, k % 2], th[:, k % 2], ACT.Copy, bias=0.5, scale=0.5).then_inc(cw_ready, 1)

            def back(b, k):
                act.wait_ge(y1_ready, b + 1)
                act.wait_ge(cw_ready, b + 1)
                if k >= 2:
                    act.wait_ge(added, (b - 1) * 32)
                for j in range(J):
                    act.activation(y2[:, k % 2, j], y1[:, k % 2, j], ACT.Copy, scale=cw[:, k % 2, j:j + 1]).then_inc(y2_ready, 1)
            split_hi(0, 0)
            split_hi(1, 1)
            phase_b(act, front, back)

        @block.vector
        def _(dve):
            n = [0]

            def put(ins):
                ins.then_inc(const_dve, 1)
                n[0] += 1
                dve.wait_ge(const_dve, n[0])
            put(dve.memset(eps[:], EPS))
            dve.memset(Macc[:], 0.0)
            dve.memset(ones8[:], 1.0)
            dve.memset(bias_rows[:], 0.0)
            dve.wait_ge(adj_in, 16 * 2)
            dve.tensor_reduce(deg[:, 0, 0:J], adj_n[:], AX.X, ALU.add)
            dve.wait_ge(degree_ready, 1)
            put(dve.tensor_copy(deg[:, 0, J:], bank[7][:, 0:NODES]))
            dve.tensor_scalar(deg[:, 1], deg[:, 0], 0.0, None, ALU.is_gt)
            put(dve.tensor_scalar(deg[:, 0], deg[:, 0], 1e-37, None, ALU.max))
            dve.wait_ge(small_in, 16 * 4)
            put(dve.tensor_copy(bias_part[:, 0], bg[:]))
            put(dve.tensor_tensor(bias_rest[:], bg[:], bias_part[:, 0], ALU.subtract))
            put(dve.tensor_copy(bias_part[:, 1], bias_rest[:]))
            put(dve.tensor_tensor(bias_part[:, 2], bias_rest[:], bias_part[:, 1], ALU.subtract))
            for k in range(3):
                dve.tensor_copy(bias_rows[32 * k:32 * k + 1], bias_part[32 * k:32 * k + 1, k])
            dve.wait_ge(deg_root, 1)
            put(dve.reciprocal(deg[:, 0], deg[:, 0]))
            put(dve.tensor_tensor(deg[:, 0], deg[:, 0], deg[:, 1], ALU.mult))
            for j in range(J):
                dve.scalar_tensor_tensor(At[:, j], At[:, j], deg[:, 0, j:j + 1], deg[:, 0, J:], ALU.mult, ALU.mult)
            dve.wait_ge(const_pool, 13)
            dve.tensor_copy(rev[:], iota_i[:, 0])
            dve.tensor_scalar(pad_out[:], pad_ids, BLOCK - 1, TOKENS, ALU.bitwise_and, ALU.bitwise_or).then_inc(pad_out_ready, 1)
            dve.tensor_copy(ebase[:], iota_i[:, 1])
            put(dve.tensor_copy(steps_f[:], steps_i[:]))

            def bc(ap):
                return ap.rearrange("p (t o) -> p t o", o=1).broadcast_to([P, TILES, E])

            def route_and_scales(g, q, e, x):
                r, z = g is not None, e is not None

                def routed(k):
                    dve.wait_ge(route, g * NROUTE + k)

                def scaled(k):
                    dve.wait_ge(scale, e * NCHAIN + k)
                L = lg[:, q]
                if r:
                    dve.tensor_reduce(m12[:, 0], L, AX.X, ALU.max).then_inc(route, 1)
                if z:
                    kk = K[:, bass.ds(e, 1)].rearrange("p a c -> p (a c)")
                    dve.wait_ge(ar_ready, e + 1)
                    dve.tensor_reduce(v[:, 2:3], ar[:, x, 2:4], AX.X, ALU.max)
                    dve.tensor_reduce(v[:, 0:1], ar[:, x, 0:2], AX.X, ALU.max).then_inc(scale, 1)
                if r:
                    routed(1)
                    dve.tensor_tensor(ra[:, 0], L, bc(m12[:, 0]), ALU.is_equal).then_inc(route, 1)
                if z:
                    scaled(1)
                    dve.tensor_scalar(v[:, 1:2], v[:, 0:1], float(D), ar[:, x, 4:5], ALU.mult, ALU.add).then_inc(scale, 1)
                if r:
                    routed(2)
                    dve.tensor_tensor(ra[:, 0], ra[:, 0], rev[:], ALU.mult).then_inc(route, 1)
                if z:
                    scaled(2)
                    dve.tensor_tensor(v[:, 1:2], v[:, 1:2], v[:, 1:2], ALU.mult).then_inc(scale, 1)
                if r:
                    routed(3)
                    dve.tensor_reduce(m12[:, 1], ra[:, 0], AX.X, ALU.max).then_inc(route, 1)
                if z:
                    scaled(3)
                    dve.tensor_scalar(v[:], v[:], 1e-30, None, ALU.max).then_inc(scale, 1)
                if r:
                    routed(4)
                    dve.tensor_tensor(ra[:, 1], rev[:], bc(m12[:, 1]), ALU.is_equal).then_inc(route, 1)
                if z:
                    scaled(4)
                    dve.tensor_scalar(pw[:].bitcast(I32), v[:].bitcast(I32), 0x7F800000, None, ALU.bitwise_and).then_inc(scale, 1)
                if r:
                    routed(5)
                    dve.scalar_tensor_tensor(ra[:, 2], ra[:, 1], -3e38, L, ALU.mult, ALU.add).then_inc(route, 1)
                if z:
                    scaled(5)
                    dve.reciprocal(rp[:], pw[:]).then_inc(scale, 1)
                if r:
                    routed(6)
                    dve.tensor_reduce(m12[:, 2], ra[:, 2], AX.X, ALU.max).then_inc(route, 1)
                if z:
                    scaled(6)
                    dve.tensor_scalar(kk[:, S1:S1 + 1], rp[:, 0:1], TOP, None, ALU.mult).then_inc(scale, 1)
                    dve.tensor_scalar(kk[:, S2:S2 + 1], rp[:, 2:3], TOP, None, ALU.mult)
                if r:
                    routed(7)
                    dve.tensor_tensor(ra[:, 0], ra[:, 2], bc(m12[:, 2]), ALU.is_equal).then_inc(route, 1)
                if z:
                    dve.tensor_scalar(kk[:, I1:I1 + 1], pw[:, 0:1], 1.0 / TOP, None, ALU.mult)
                    dve.tensor_tensor(kk[:, C2:C2 + 1], pw[:, 0:1], rp[:, 1:2], ALU.mult)
                if r:
                    routed(8)
                    dve.tensor_tensor(ra[:, 0], ra[:, 0], rev[:], ALU.mult).then_inc(route, 1)
                if z:
                    dve.scalar_tensor_tensor(kk[:, CY:CY + 1], pw[:, 1:2], TOP ** -2, pw[:, 2:3], ALU.mult, ALU.mult)
                    scaled(7)
                    dve.tensor_scalar(beta[:, bass.ds(e, 1)].rearrange("p a f -> p (a f)"),
                                      b1t[:, bass.ds(e, 1), HK:].rearrange("p a f -> p (a f)"), kk[:, S1:S1 + 1], None,
                                      ALU.mult).then_inc(scale, 1)
                if r:
                    routed(9)
                    dve.tensor_reduce(m12[:, 3], ra[:, 0], AX.X, ALU.max).then_inc(route, 1)
                    routed(10)
                    dve.tensor_tensor(ra[:, 3], rev[:], bc(m12[:, 3]), ALU.is_equal).then_inc(route, 1)
                    dve.tensor_tensor(m12[:, 4], m12[:, 0], m12[:, 2], ALU.subtract)
                    routed(11)
                    dve.tensor_tensor(M[:, q], ra[:, 1], ra[:, 3], ALU.add).then_inc(route, 1)
                    dve.tensor_tensor(ra[:, 4], ra[:, 1], ra[:, 3], ALU.subtract).then_inc(route, 1)
                    routed(13)
                    dve.tensor_tensor(xrow[:, q * GROUP:(q + 1) * GROUP, :, D:].rearrange("p b j e -> p (b j) e"),
                                      ra[:, 4], bc(m12[:, 4]), ALU.mult).then_inc(route, 1)

            def route_2(g, q):
                dve.wait_ge(rank_ready, g + 1)
                dve.tensor_reduce(Mg[:], M[:, q].rearrange("p t e -> p e t"), AX.X, ALU.add).then_inc(route, 1)
                dve.tensor_tensor(ra[:, 5], rkp, ebase[:], ALU.add).then_inc(route, 1)
                dve.wait_ge(route, g * NROUTE + 16)
                dve.tensor_tensor(Macc[:, 1 - q], Macc[:, q], Mg[:], ALU.add)
                dve.tensor_copy(gids[:, q], ids[:, bass.ds(g * TILES, TILES)])
                dve.tensor_tensor(ra[:, 1], ra[:, 1], ra[:, 5], ALU.mult)
                dve.tensor_tensor(ra[:, 3], ra[:, 3], ra[:, 5], ALU.mult).then_inc(route, 1)
                dve.wait_ge(route, g * NROUTE + 17)
                with nc.allow_low_precision("places are integers below 2**17, exact in float32"):
                    dve.tensor_reduce(slots[:, q, 0], ra[:, 1], AX.X, ALU.add)
                    dve.tensor_reduce(slots[:, q, 1], ra[:, 3], AX.X, ALU.add).then_inc(route, 1)

            def split_lo(b, k):
                dve.wait_ge(hi_ready, b + 1)
                dve.tensor_tensor(parts[:, k % 2, :, D:], G[:, k % 4, :, 0:D], parts[:, k % 2, :, 0:D], ALU.subtract).then_inc(lo_ready, 1)

            def xt(b, k):
                dve.wait_ge(XTp_ready, b + 1)
                if k >= 2:
                    dve.wait_ge(h_ready, (b - 1) * HK)
                dve.tensor_copy(XT[:, k % 2], xTp).then_inc(XT_ready, 1)

            listing = [0]

            def go(ins):
                ins.then_inc(blk, 1)
                listing[0] += 1
                dve.wait_ge(blk, listing[0])

            def over_blocks(ap, m):
                return ap.rearrange("p (a e) -> p a e", a=1).broadcast_to([1, m, E])

            def over_experts(ap, m):
                return ap.rearrange("p (b a) -> p b a", a=1).broadcast_to([1, m, E])
            length, filled, filled_to, following, total, blocks, left, left_to, lag = (nb[:, n] for n in range(9))
            each = steps_f[:, 0:32].rearrange("p (a s) -> p a s", a=1).broadcast_to([1, E, 32])

            def list_early():
                dve.wait_ge(tot_ready, 1)
                dve.memset(following, 0.0)
                go(dve.tensor_copy(length, totp[0:1, 0]))
                go(dve.tensor_tensor(cmp1, length.rearrange("p (e a) -> p e a", a=1).broadcast_to([1, E, 32]), each, ALU.is_ge))
                go(dve.tensor_reduce(total, cmp1, AX.X, ALU.add))
                go(dve.tensor_scalar(filled, total, -1.0, None, ALU.add))
                dve.tensor_copy(following[:, 0:E - 1], filled[:, 1:E])
                go(dve.tensor_tensor_scan(filled_to, ones8[:], filled, 0.0, ALU.mult, ALU.add))
                go(dve.tensor_tensor(cmp2, over_experts(steps_f[:, 32:], MAX_BLOCKS), over_blocks(filled_to, MAX_BLOCKS), ALU.is_ge))
                go(dve.tensor_reduce(early[:, 0], cmp2, AX.X, ALU.add))
                go(dve.tensor_tensor(cmp2, cmp2, over_blocks(filled, MAX_BLOCKS), ALU.mult))
                go(dve.tensor_reduce(bl[:, 0], cmp2, AX.X, ALU.add))
                go(dve.tensor_tensor(bl[:, 1], steps_f[:, 32:], bl[:, 0], ALU.subtract))
                go(dve.scalar_tensor_tensor(early[:, 1], early[:, 0], float(TOKENS // BLOCK), bl[:, 1], ALU.mult, ALU.add))
                dve.tensor_copy(info[:, :, 0:EARLY_BLOCKS], early[:, :, 0:EARLY_BLOCKS]).then_inc(early_listed, 1)

            def list_late_1():
                m = LATE_BLOCKS
                later = cmp2[:, 0:m]
                dve.wait_ge(tot_ready, 2)
                go(dve.tensor_copy(length, totp[0:1, 1]))
                go(dve.tensor_tensor(cmp1, length.rearrange("p (e a) -> p e a", a=1).broadcast_to([1, E, 32]), each, ALU.is_gt))
                dve.tensor_scalar(bl[:, 2, 0:m], steps_f[:, 32 + EARLY_BLOCKS:], filled_to[:, E - 1:E], None, ALU.subtract)
                go(dve.tensor_reduce(blocks, cmp1, AX.X, ALU.add))
                dve.tensor_tensor(lag, blocks, following, ALU.subtract)
                go(dve.tensor_tensor(left, blocks, filled, ALU.subtract))
                go(dve.tensor_tensor_scan(left_to, ones8[:], left, 0.0, ALU.mult, ALU.add))
                go(dve.tensor_tensor(later, over_experts(bl[:, 2, 0:m], m), over_blocks(left_to, m), ALU.is_ge))
                go(dve.tensor_reduce(bl[:, 0, 0:m], later, AX.X, ALU.add))

            def list_late_2():
                m = LATE_BLOCKS
                later = cmp2[:, 0:m]
                go(dve.tensor_tensor(later, later, over_blocks(lag, m), ALU.mult))
                go(dve.tensor_reduce(bl[:, 1, 0:m], later, AX.X, ALU.add))
                go(dve.scalar_tensor_tensor(late[:, 1, 0], bl[:, 2, 0:m], filled[:, 0:1], bl[:, 1, 0:m], ALU.add, ALU.subtract))
                dve.tensor_scalar(late[:, 0, 0], bl[:, 0, 0:m], float(E - 1), None, ALU.min)
                dve.tensor_scalar(late[:, 2, 0], bl[:, 2, 0:m], 0.0, None, ALU.is_lt)
                dve.tensor_scalar(late[:, 2, 1], bl[:, 2, 0:m], 0.0, None, ALU.is_lt)
                go(dve.scalar_tensor_tensor(late[:, 0, 1], bl[:, 0, 0:m], float(TOKENS // BLOCK), late[:, 1, 0], ALU.mult, ALU.add))
                go(dve.tensor_tensor(late[:, 1], early[:, :, EARLY_BLOCKS:], late[:, 0], ALU.subtract))
                go(dve.tensor_tensor(late[:, 1], late[:, 1], late[:, 2], ALU.mult))
                dve.memset(info[:, :, MAX_BLOCKS:], 0)
                dve.tensor_tensor(info[:, :, EARLY_BLOCKS:MAX_BLOCKS], late[:, 1], late[:, 0], ALU.add).then_inc(listed, 1)

            def step(i, s, g):
                p = s % 2
                if live(s, 0):
                    dve.wait_ge(x_in[s % 4], (i - s % 4) * 4 + 16)
                    for j in range(J):
                        dve.bn_stats(st[:, p, j], xin[:, s % 4, j]).then_inc(bn1, 1)
                if live(s, 2):
                    dve.wait_ge(g_ready, i - 1)
                    if s >= 6:
                        dve.wait_ge(x2_stored[(s - 2) % 4], (i - 2 - (s - 2) % 4) * 4)
                    if s >= 6:
                        dve.wait_ge(xn2_ready, (i - 5) * J)
                    dve.tensor_tensor(x2[:, (s - 2) % 4], g_bank(s % 2), xin[:, (s - 2) % 4], ALU.add).then_inc(x2_ready, 1)
                if live(s, 0):
                    hold(dve, bn1, (i + 1) * J)
                    for j in range(J):
                        dve.bn_aggr(mv[:, p, j], st[:, p, j]).then_inc(mv1, 1)
                if live(s, 2):
                    dve.wait_ge(x2_ready, i - 1)
                    for j in range(J):
                        dve.bn_stats(st[:, p, J + j], x2[:, (s - 2) % 4, j]).then_inc(bn2, 1)
                if live(s, 5):
                    c = (s - 5) % GROUP * J
                    dve.wait_ge(lgp_ready, i - 4)
                    dve.tensor_tensor(lg[:, ((s - 5) // GROUP) % 2, c:c + J], lgp,
                                      rb[:].rearrange("p (a e) -> p a e", a=1).broadcast_to([P, J, E]), ALU.add).then_inc(lg_ready, 1)
                if live(s, 2):
                    hold(dve, bn2, (i - 1) * J)
                    for j in range(J):
                        dve.bn_aggr(mv[:, p, J + j], st[:, p, J + j]).then_inc(mv2, 1)
                if s % GROUP >= 2 and live(s - s % GROUP, 4):
                    q, u, e = (s // GROUP - 1) % 2, s % GROUP - 2, g - 1
                    for k, (dst, c, a, n) in enumerate(((w1_half, S1, 0, W1N // 2), (w2_half, S2, W1N, W2N // 2))):
                        dve.wait_ge(whi_ready, e * 4 + 2 * u + k + 1)
                        dve.scalar_tensor_tensor(dst(e, 1, u), stage[:, q, a + u * n:a + (u + 1) * n], kcol(e, c),
                                                 dst(e, 0, u), ALU.mult, ALU.subtract).then_inc(wlo_ready, 1)
                if s % GROUP == 1 and live(s, 9):
                    dve.wait_ge(scattered[(s // GROUP) % 2], parcount(g, s))
                    route_2(g - 2, (s // GROUP) % 2)
                if live(s, 0) or live(s, 2):
                    a, z = (0 if live(s, 0) else J), (2 * J if live(s, 2) else J)
                    dve.wait_ge(sd_ready, i + 1)
                    dve.reciprocal(rs[:, p, a:z], sd[:, p, a:z]).then_inc(rs_ready, 1)
                    dve.wait_ge(rs_ready, i + 1)
                    dve.scalar_tensor_tensor(nmr[:, p, a:z], mv[:, p, a:z, 0], -1.0, rs[:, p, a:z], ALU.mult, ALU.mult).then_inc(nmr_ready, 1)
                if s == LAST - 1:
                    dve.wait_ge(early_listed, 1)
                    split_lo(0, 0)
                    split_lo(1, 1)
                    xt(0, 0)
                if s % GROUP == 0:
                    if live(s, 8):
                        dve.wait_ge(lg_ready, (g - 1) * GROUP)
                    if live(s, 8) or live(s, 4):
                        route_and_scales(g - 2 if live(s, 8) else None, (s // GROUP) % 2,
                                         g - 1 if live(s, 4) else None, (s // GROUP - 1) % 2)
                if s == EARLY * GROUP + 9:
                    list_early()
                if live(s, 0) and s % GROUP >= 2:
                    q, u = (s // GROUP) % 2, s % GROUP - 2
                    dve.wait_ge(w_in[q], (g - q) * 32 + 32 * (u + 1))
                    if u == 0:
                        if s == 2:
                            dve.wait_ge(expert_in, 16 * 2)
                        if s >= 8:
                            dve.wait_ge(ar_ready, g - 1)
                        dve.tensor_reduce(am[:, q, 4:5], b1t[:, bass.ds(g, 1)].rearrange("p a f -> p (a f)"), AX.X, ALU.max,
                                          apply_absolute_value=True).then_inc(am_ready, 1)
                    dve.tensor_reduce(am[:, q, u:u + 1], stage[:, q, u * 1024:(u + 1) * 1024], AX.X, ALU.max,
                                      apply_absolute_value=True).then_inc(am_ready, 1)

            def parcount(g, s):
                q = (s // GROUP) % 2
                return (g - 2 - q) * (16 * 2 * TILES // 2) + 16

            phase_a(dve, step)

            def front(b, k):
                e = dve.value_load(info[0:1, 0, bass.ds(b, 1)], min_val=0, max_val=E - 1)
                for f in range(HK):
                    dve.wait_ge(act_ready, b * HK + f + 1)
                    if k >= 2 and f == 0:
                        dve.wait_ge(ahi_ready, b - 1)
                        dve.wait_ge(alo_ready, b - 1)
                    dve.scalar_tensor_tensor(prod[:, k % 2, f], bank[f][:, BLOCK:], beta[:, bass.ds(e, 1), f:f + 1].rearrange("p a f -> p (a f)"),
                                             act1[:, f], ALU.add, ALU.mult).then_inc(prod_ready, 1)
                    if f == 1 and not (isinstance(b, int) and b + 1 >= MAX_BLOCKS):
                        xt(b + 1, k + 1)
                    if f == 2 and not (isinstance(b, int) and b + 2 >= MAX_BLOCKS):
                        split_lo(b + 2, k + 2)
                dve.wait_ge(ahi_ready, b + 1)
                dve.scalar_tensor_tensor(ab[:, k % 2, 1], prod[:, k % 2], kcol(e, C2), ab[:, k % 2, 0], ALU.mult, ALU.subtract).then_inc(alo_ready, 1)

            def back(b, k):
                e = dve.value_load(info[0:1, 0, bass.ds(b, 1)], min_val=0, max_val=E - 1)
                dve.wait_ge(y_ready, b + 1)
                if k >= 2:
                    dve.wait_ge(y2_ready, (b - 1) * J)
                dve.scalar_tensor_tensor(y1[:, k % 2], bank[5 + k % 2][:].rearrange("p (j d) -> p j d", j=J), kcol(e, CY),
                                         b2t[:, bass.ds(e, 1)].broadcast_to([P, J, D]), ALU.mult, ALU.add).then_inc(y1_ready, 1)
                if k == 0:
                    list_late_1()
                if k == 1:
                    list_late_2()
            phase_b(dve, front, back, step)

        @block.tensor
        def _(pe):
            def step(i, s, g):
                if s == 0:
                    pe.wait_ge(const_pool, 13)
                    pe.wait_ge(adj_in, 16 * 2)
                    for m in range(J):
                        mm = pe.matmul(bank[7][:, 0:NODES], ones_f[:], At[:, m], start=(m == 0), stop=(m == J - 1))
                    mm.then_inc(degree_ready, 1)
                    pe.wait_ge(const_dve, CONST_DVE)
                if s == EARLY * GROUP + 8:
                    pe.wait_ge(route, EARLY * NROUTE)
                    pe.matmul(totp[:, 0], ones[:], Macc[:, EARLY % 2], start=True, stop=True).then_inc(tot_ready, 1)
                if live(s, 2):
                    pe.wait_ge(ts_ready, i - 1)
                    if s >= 4:
                        pe.wait_ge(x2_ready, i - 3)
                    for j in range(J):
                        for k in range(DK):
                            mm = pe.matmul(g_bank(s % 2)[:, j], ts[:, s % 2, k, j * P:(j + 1) * P], Wg[:, k], start=(k == 0), stop=False)
                        mm = pe.matmul(g_bank(s % 2)[:, j], ones_b[:], bias_rows[:], start=False, stop=True)
                    mm.then_inc(g_ready, 1)
                if live(s, 5):
                    pe.wait_ge(xT_ready, i - 4)
                    if s >= 6:
                        pe.wait_ge(lg_ready, i - 5)
                    for j in range(J):
                        for k in range(DK):
                            mm = pe.matmul(lgp[:, j], xT[:, (s - 5) % 2, k, j * P:(j + 1) * P], rw[:, k], start=(k == 0), stop=(k == DK - 1))
                    mm.then_inc(lgp_ready, 1)
                if live(s, 4):
                    pe.wait_ge(xn2_ready, (i - 3) * J)
                    if s >= 5:
                        pe.wait_ge(xT_ready, i - 4)
                    for k in range(DK):
                        for j in range(J):
                            mm = pe.transpose(xnTp[:, k, j * P:(j + 1) * P], xrow[:, (s - 4) % 8, j, k * P:(k + 1) * P], ident_f[:])
                    mm.then_inc(xTp_ready, 1)
                if s % GROUP == 1 and live(s, 9):
                    q = (s // GROUP) % 2
                    pe.wait_ge(route, (g - 2) * NROUTE + 12)
                    pe.matmul(rkp, tri[:], M[:, q], start=True, stop=False)
                    pe.matmul(rkp, ones[:], Macc[:, q].rearrange("p (a e) -> p a e", a=1).broadcast_to([P, TILES, E]), start=False, stop=False)
                    for c in range(TILES - 1):
                        mm = pe.matmul(rkp[:, c + 1:], ones[:], M[:, q, c:c + 1].broadcast_to([P, TILES - 1 - c, E]),
                                       start=False, stop=(c == TILES - 2))
                    mm.then_inc(rank_ready, 1)
                if live(s, 1):
                    pe.wait_ge(xn1_ready, i * J)
                    if s >= 3:
                        pe.wait_ge(ts_ready, i - 2)
                    for t in range(DK):
                        for m in range(J):
                            mm = pe.matmul(bank[(s - 1) % 2][:, t * NODES:(t + 1) * NODES], xn1[:, (s - 1) % 2, m, t * P:(t + 1) * P],
                                           At[:, m], start=(m == 0), stop=(m == J - 1))
                    mm.then_inc(t_ready, 1)
            phase_a(pe, step)

            pe.wait_ge(early_listed, 1)
            pe.wait_ge(wlo_ready, E * 4)
            pe.wait_ge(whi_ready, E * 4)

            def rows_t(b, k):
                pe.wait_ge(hi_ready, b + 1)
                pe.wait_ge(lo_ready, b + 1)
                if k >= 1:
                    pe.wait_ge(XT_ready, b)
                for l in range(2):
                    for c in range(DK):
                        for j in range(J):
                            mm = pe.transpose(xTp[:, l, c, j * P:(j + 1) * P], parts[:, k % 2, j, l * D + c * P:l * D + (c + 1) * P], ident[:])
                mm.then_inc(XTp_ready, 1)

            def front(b, k):
                e = pe.value_load(info[0:1, 0, bass.ds(b, 1)], min_val=0, max_val=E - 1)
                pe.wait_ge(XT_ready, b + 1)
                for f in range(HK):
                    if k >= 1:
                        pe.wait_ge(prod_ready, (b - 1) * HK + f + 1)
                    for half in range(2):
                        n = 0
                        for c in range(DK):
                            for lw in range(2):
                                w = W1[:, bass.ds(e, 1), lw, c, half * H + f * P:half * H + (f + 1) * P].rearrange("p a n -> p (a n)")
                                for lx in range(2 - lw):
                                    mm = pe.matmul(bank[f][:, half * BLOCK:(half + 1) * BLOCK], w, XT[:, k % 2, lx, c], start=(n == 0), stop=(n == 5))
                                    n += 1
                    mm.then_inc(h_ready, 1)
                    if f == 1 and not (isinstance(b, int) and b + 1 >= MAX_BLOCKS):
                        rows_t(b + 1, k + 1)

            def back(b, k):
                if k == 0:
                    pe.wait_ge(route, GROUPS * NROUTE)
                    pe.matmul(totp[:, 1], ones[:], Macc[:, GROUPS % 2], start=True, stop=True).then_inc(tot_ready, 1)
                e = pe.value_load(info[0:1, 0, bass.ds(b, 1)], min_val=0, max_val=E - 1)
                pe.wait_ge(ahi_ready, b + 1)
                pe.wait_ge(alo_ready, b + 1)
                if k >= 2:
                    pe.wait_ge(y1_ready, b - 1)
                n = 0
                for j in range(J):
                    n = 0
                    for c in range(HK):
                        for lw in range(2):
                            w = W2[:, bass.ds(e, 1), lw, c].rearrange("p a n -> p (a n)")
                            for la in range(2 - lw):
                                mm = pe.matmul(bank[5 + k % 2][:, j * D:(j + 1) * D], ab[:, k % 2, la, c, j * P:(j + 1) * P], w,
                                               start=(n == 0), stop=(n == 3 * HK - 1))
                                n += 1
                mm.then_inc(y_ready, 1)
            rows_t(0, 0)
            phase_b(pe, front, back, step)


def kernel(x, adj, L0_gnn_weight, L0_gnn_bias, L0_ffn_router_w, L0_ffn_router_b, L0_ffn_fc1_w, L0_ffn_fc1_b,
           L0_ffn_fc2_w, L0_ffn_fc2_b):
    import numpy as np
    import concourse.bacc as bacc
    from concourse.bass_utils import run_bass_kernel_spmd

    def tiles(a):
        a = np.asarray(a)
        return np.ascontiguousarray(a.reshape(a.shape[0] // P, P, a.shape[1]).transpose(1, 0, 2))

    fc1 = np.asarray(L0_ffn_fc1_w)
    fc2 = np.asarray(L0_ffn_fc2_w)
    arrays = {
        "x": np.ascontiguousarray(np.asarray(x).reshape(TOKENS, D)),
        "adj": tiles(adj),
        "adj_t": tiles(np.asarray(adj).T),
        "gnn_w": tiles(L0_gnn_weight),
        "gnn_b": np.asarray(L0_gnn_bias),
        "router_w": tiles(np.asarray(L0_ffn_router_w).T),
        "router_b": np.asarray(L0_ffn_router_b),
        "w1": np.ascontiguousarray(fc1.reshape(E, 2 * H, DK, P).transpose(0, 3, 2, 1).reshape(E, P, W1N)),
        "b1": np.ascontiguousarray(np.asarray(L0_ffn_fc1_b).reshape(E, FT, P).transpose(2, 0, 1)),
        "w2": np.ascontiguousarray(fc2.reshape(E, D, HK, P).transpose(0, 3, 2, 1).reshape(E, P, W2N)),
        "b2": np.asarray(L0_ffn_fc2_b),
    }
    nc = bacc.Bacc("TRN2", target_bir_lowering=False, num_devices=1)
    feed, args = {}, []
    for name, a in arrays.items():
        feed[f"in_{name}"] = a
        args.append(nc.dram_tensor(f"in_{name}", a.shape, mybir.dt.from_np(a.dtype), kind="ExternalInput").ap())
    out = nc.dram_tensor("out", (TOKENS + BLOCK, D), F32, kind="ExternalOutput").ap()
    program(nc, *args, out)
    r = run_bass_kernel_spmd(nc, [feed], core_ids=[0])
    return r.results[0]["out"][:TOKENS].reshape(BATCHES, NODES, D)
```
